# Optimizing a Trainium2 kernel written in Bass

```python
import numpy as np
import jax
import jax.numpy as jnp

def _softmax(x, axis=-1):
    return jax.nn.softmax(x, axis=axis)

def _gelu(x):
    return jax.nn.gelu(x, approximate=True)

def _silu(x):
    return jax.nn.silu(x)

def _sigmoid(x):
    return jax.nn.sigmoid(x)

def _layernorm(x, axis=-1, eps=1e-05):
    m = jnp.mean(x, axis=axis, keepdims=True)
    v = jnp.var(x, axis=axis, keepdims=True)
    return (x - m) / jnp.sqrt(v + eps)

def _scatter_add(tgt, idx, src, axis=0):
    return tgt.at[idx].add(src)

def _segment_sum(src, seg, n):
    return jax.ops.segment_sum(src, seg, n)
kernel_name = 'mk_adj_preln_d2_adj_r2_860890'

def setup_inputs(seed: int=0):
    np.random.seed(seed)
    _w = jnp.asarray

    def _rec_inputs():
        import jax
        import jax.numpy as jnp
        _gk = jax.random.key(seed)
        x = -0.0002928 + 1 * jax.random.normal(jax.random.fold_in(_gk, 1), (2048, 256), jnp.float32)
        _a = jax.random.bernoulli(jax.random.fold_in(_gk, 2), 0.0078125, (2048, 2048))
        _a = jnp.logical_or(_a, jnp.swapaxes(_a, -1, -2))
        _a = jnp.logical_or(_a, jnp.eye(2048, dtype=bool))
        _af = _a.astype(jnp.float32)
        _af = _af * jax.random.uniform(jax.random.fold_in(_gk, 3), (2048, 2048), jnp.float32, 0.05, 1)
        adj = _af
        return (x, adj)
    x, adj = _rec_inputs()

    def _L0_gnn_setup():
        import jax, jax.numpy as jnp
        import numpy as np
        N, IN_DIM, OUT_DIM = (4096, 256, 256)
        ALPHA = 0.2
        EPS = 1e-09
        key = jax.random.key(seed)
        k1, k2, k3, k4, k5 = jax.random.split(key, 5)
        feat = jax.random.normal(k1, (N, IN_DIM), dtype=jnp.float32)
        counting_attn = jax.random.uniform(k2, (N, N), dtype=jnp.float32)
        W = jax.random.normal(k3, (IN_DIM, OUT_DIM), dtype=jnp.float32) / np.sqrt(IN_DIM)
        attn_l = jax.random.normal(k4, (OUT_DIM, 1), dtype=jnp.float32) * 0.1
        attn_r = jax.random.normal(k5, (OUT_DIM, 1), dtype=jnp.float32) * 0.1
        return {'feat': feat, 'counting_attn': counting_attn, 'W': W, 'attn_l': attn_l, 'attn_r': attn_r}
    _L0_gnn_all = _L0_gnn_setup()
    _L0_gnn_in = {k: v for k, v in _L0_gnn_all.items() if k in ('W', 'attn_l', 'attn_r')}
    del _L0_gnn_all

    def _L1_gnn_setup():
        import jax, jax.numpy as jnp
        import numpy as np
        N, D_IN, D_ATTN, STEPS, P_NUC, TAU = (2048, 256, 64, 2, 0.9, 1.0)
        LN_EPS = 1e-05

        def _xavier(key, shape):
            fan_in, fan_out = (shape[-2], shape[-1])
            lim = np.sqrt(6.0 / (fan_in + fan_out))
            return jax.random.uniform(key, shape, jnp.float32, -lim, lim)

        def _adj_from_feats(Xa, W1, W2, W3):
            Q = Xa @ W1
            K = Xa @ W3
            logits = Q @ W2 @ K.T / TAU
            idx = jnp.argsort(-logits, axis=1)
            vals = jnp.take_along_axis(logits, idx, axis=1)
            csum = jnp.cumsum(jax.nn.softmax(vals, axis=1), axis=1)
            k_i = jnp.sum(csum < P_NUC, axis=1) + 1
            ranks = jnp.arange(logits.shape[1])[None, :]
            keep_sorted = ranks < k_i[:, None]
            inv = jnp.argsort(idx, axis=1)
            keep = jnp.take_along_axis(keep_sorted, inv, axis=1)
            masked = jnp.where(keep, logits, -jnp.inf)
            return jax.nn.softmax(masked, axis=1)
        key = jax.random.key(seed)
        ks = jax.random.split(key, 9)
        return {'X': jax.random.normal(ks[0], (N, D_IN), jnp.float32), 'S': jax.random.uniform(ks[1], (N, N), jnp.float32), 'W1': _xavier(ks[2], (D_IN, D_ATTN)), 'W2': _xavier(ks[3], (D_ATTN, D_ATTN)), 'W3': _xavier(ks[4], (D_IN, D_ATTN)), 'U1': _xavier(ks[5], (STEPS, D_IN, D_IN)), 'U2': _xavier(ks[6], (STEPS, D_IN, D_IN)), 'U3': _xavier(ks[7], (STEPS, D_IN, D_IN)), 'gamma': jnp.ones((D_IN,), jnp.float32), 'beta': jnp.zeros((D_IN,), jnp.float32)}
    _L1_gnn_all = _L1_gnn_setup()
    _L1_gnn_in = {k: v for k, v in _L1_gnn_all.items() if k in ('W1', 'W2', 'W3', 'U1', 'U2', 'U3', 'gamma', 'beta')}
    del _L1_gnn_all
    return {'x': x, 'adj': adj, 'L0_gnn_W': _L0_gnn_in['W'], 'L0_gnn_attn_l': _L0_gnn_in['attn_l'], 'L0_gnn_attn_r': _L0_gnn_in['attn_r'], 'L1_gnn_W1': _L1_gnn_in['W1'], 'L1_gnn_W2': _L1_gnn_in['W2'], 'L1_gnn_W3': _L1_gnn_in['W3'], 'L1_gnn_U1': _L1_gnn_in['U1'], 'L1_gnn_U2': _L1_gnn_in['U2'], 'L1_gnn_U3': _L1_gnn_in['U3'], 'L1_gnn_gamma': _L1_gnn_in['gamma'], 'L1_gnn_beta': _L1_gnn_in['beta']}

def reference(x, adj, L0_gnn_W, L0_gnn_attn_l, L0_gnn_attn_r, L1_gnn_W1, L1_gnn_W2, L1_gnn_W3, L1_gnn_U1, L1_gnn_U2, L1_gnn_U3, L1_gnn_gamma, L1_gnn_beta):
    import jax
    import jax.numpy as jnp

    def _L0_gnn_ref(feat, counting_attn, W, attn_l, attn_r):
        import jax, jax.numpy as jnp
        import numpy as np
        N, IN_DIM, OUT_DIM = (4096, 256, 256)
        ALPHA = 0.2
        EPS = 1e-09
        h = feat @ W
        a1 = h @ attn_l
        a2 = h @ attn_r
        a = jax.nn.leaky_relu(a1 + a2.T, ALPHA)
        a = a - jnp.max(a, axis=1, keepdims=True)
        nomi = jnp.exp(a) * counting_attn
        deno = jnp.sum(nomi, axis=1, keepdims=True)
        a_nor = nomi / (deno + EPS)
        ret = jax.nn.elu(a_nor @ h)
        return ret

    def _L1_gnn_ref(X, S, W1, W2, W3, U1, U2, U3, gamma, beta):
        import jax, jax.numpy as jnp
        import numpy as np
        N, D_IN, D_ATTN, STEPS, P_NUC, TAU = (2048, 256, 64, 2, 0.9, 1.0)
        LN_EPS = 1e-05

        def _xavier(key, shape):
            fan_in, fan_out = (shape[-2], shape[-1])
            lim = np.sqrt(6.0 / (fan_in + fan_out))
            return jax.random.uniform(key, shape, jnp.float32, -lim, lim)

        def _adj_from_feats(Xa, W1, W2, W3):
            Q = Xa @ W1
            K = Xa @ W3
            logits = Q @ W2 @ K.T / TAU
            idx = jnp.argsort(-logits, axis=1)
            vals = jnp.take_along_axis(logits, idx, axis=1)
            csum = jnp.cumsum(jax.nn.softmax(vals, axis=1), axis=1)
            k_i = jnp.sum(csum < P_NUC, axis=1) + 1
            ranks = jnp.arange(logits.shape[1])[None, :]
            keep_sorted = ranks < k_i[:, None]
            inv = jnp.argsort(idx, axis=1)
            keep = jnp.take_along_axis(keep_sorted, inv, axis=1)
            masked = jnp.where(keep, logits, -jnp.inf)
            return jax.nn.softmax(masked, axis=1)
        n = X.shape[0]
        S = S + jnp.eye(n, dtype=X.dtype)
        Rf = S / jnp.clip(S.sum(axis=1, keepdims=True), 1e-12)
        Rb = S / jnp.clip(S.sum(axis=0), 1e-12)[:, None]
        Xf, Xb, Xa = (X, X, X)
        Z = jnp.zeros_like(X)
        for s in range(STEPS):
            A = _adj_from_feats(Xa, W1, W2, W3)
            Xf = Rf @ Xf
            Xb = Rb @ Xb
            Xa = A @ Xa
            Z = Z + (Xf @ U1[s] + Xb @ U2[s] + Xa @ U3[s])
        Y = X + Z
        mu = Y.mean(axis=-1, keepdims=True)
        var = Y.var(axis=-1, keepdims=True)
        return (Y - mu) / jnp.sqrt(var + LN_EPS) * gamma + beta
    h = jnp.maximum(_layernorm(x, axis=-1), 0.0)
    x = x + _L0_gnn_ref(h, adj, L0_gnn_W, L0_gnn_attn_l, L0_gnn_attn_r)
    h = jnp.maximum(_layernorm(x, axis=-1), 0.0)
    x = x + _L1_gnn_ref(h, adj, L1_gnn_W1, L1_gnn_W2, L1_gnn_W3, L1_gnn_U1, L1_gnn_U2, L1_gnn_U3, L1_gnn_gamma, L1_gnn_beta)
    return x

_drawn_inputs = setup_inputs


def setup_inputs(seed=0):
    import zlib

    import numpy as np

    out = dict(_drawn_inputs(seed))
    spreads = {'L1_gnn_gamma': (1.0, 0.2), 'L1_gnn_beta': (0.0, 0.1)}
    factors = {}
    for name, (base, spread) in spreads.items():
        noise = np.random.default_rng([zlib.crc32(name.encode()), seed]).standard_normal(out[name].shape)
        drawn = base * np.exp(spread * noise) if base else spread * noise
        out[name] = jnp.asarray(drawn.astype(out[name].dtype))
    for name, factor in factors.items():
        out[name] = (out[name] * factor).astype(out[name].dtype)
    return out
```

```python
import concourse.bass as bass
import concourse.mybir as mybir
from concourse.alu_op_type import AluOpType as ALU

N = 2048
D = 256
DA = 64
P = 128
NT = N // P
KD = D // P
BANK = 512
NQ = N // BANK
ALPHA = 0.2
EPS_ATT = 1e-9
EPS_LN = 1e-5
P_NUC = 0.9

LOG2_RANGE = 15.0
STEPS = 20
RATIO = [2.0 ** (LOG2_RANGE / 2 ** (k + 1)) for k in range(STEPS)]
LOW_END = (1 - P_NUC) / N * (1 - 1e-5)
SLOTS = 4


def order_of_step(step):
    tasks = [("logits", t) for t in range(SLOTS)]
    if step == 0:
        side = [("spread", t) for t in range(NT)] + [("second", t) for t in range(NT)]
        for _ in range(8):
            tasks.append(side.pop(0))
    else:
        side = []
    for t in range(NT):
        tasks.append(("flip", t))
        if t + SLOTS < NT:
            tasks.append(("logits", t + SLOTS))
        tasks.append(("mix", t))
        for _ in range(3 if t % 2 else 0):
            if side:
                tasks.append(side.pop(0))
    return tasks + side


ORDER = [order_of_step(0), order_of_step(1)]


def search_units():
    half = STEPS // 2
    units = []
    pairs = NT // 2

    def start(q):
        return [("max", 2 * q), ("max", 2 * q + 1), ("begin", q)]

    units += start(0)
    units += [("probe", 0, k) for k in range(half)]
    units += start(1)
    for q in range(pairs):
        for k in range(half):
            units.append(("probe", q, half + k))
            if q + 1 < pairs:
                units.append(("probe", q + 1, k))
        units.append(("keep", q))
        if q + 2 < pairs:
            units += [("max", 2 * q + 4), ("max", 2 * q + 5), ("begin", q + 2)]
    return units


class Tally:

    def __init__(self, sem):
        self.sem, self.n = sem, 0

    def on(self, ins, by=1):
        self.n += by
        ins.then_inc(self.sem, by)
        return self.n


def build(nc, x, adj, W, attn_l, attn_r, W1, W2, W3, U1, U2, U3, gamma, beta, out):
    from contextlib import ExitStack
    f32 = mybir.dt.float32
    ACT = mybir.ActivationFunctionType
    AX = mybir.AxisListType.X

    adjT_dram = nc.dram_tensor("adjT_scratch", [NT, P, NT * P], f32, kind="Internal").ap()
    x1_dram = nc.dram_tensor("x1_scratch", [P, NT * D], f32, kind="Internal").ap()
    rows = lambda ap: ap.rearrange("(t p) d -> p t d", p=P)

    with ExitStack() as ctx:
        def sb(name, shape):
            return ctx.enter_context(nc.sbuf_tensor(name, shape, f32))

        def sem(name):
            return ctx.enter_context(nc.semaphore(name))

        ident = sb("ident", [P, P])
        ones = sb("ones", [P, 2])
        Xn = sb("Xn", [P, NT, D])
        XT = sb("XT", [P, KD, N])
        Xb = sb("Xb", [P, NT, D])
        W1s = sb("W1s", [P, KD, DA])
        W1T = sb("W1T", [DA, D])
        W12 = sb("W12", [P, KD, DA])
        W2s = sb("W2s", [DA, DA])
        W3s = sb("W3s", [P, KD, DA])
        U12s = sb("U12s", [P, KD, 2, 2 * D])
        U3s = sb("U3s", [P, KD, 2 * D])
        gam = sb("gam", [P, D])
        bet = sb("bet", [P, D])
        st6 = sb("st6", [P, NT, 6])
        mv = sb("mv", [P, NT, 2])
        ve = sb("ve", [P, NT])
        sd = sb("sd", [P, NT])
        y0 = sb("y0", [P, NT])
        yt = sb("yt", [P, NT])
        rstd = sb("rstd", [P, NT])
        nmr = sb("nmr", [P, NT])
        a2max = sb("a2max", [P, 1])
        sm = sb("sm", [P, NT])
        sm2 = sb("sm2", [P, NT])
        off1 = sb("off1", [P, NT])
        off2 = sb("off2", [P, NT])
        deno = sb("deno", [P, NT])
        rden = sb("rden", [P, NT])
        rsum = sb("rsum", [P, NT])
        rinv = sb("rinv", [P, NT])
        csum = sb("csum", [P, NT])
        cinv = sb("cinv", [P, NT])
        nmax = sb("nmax", [P, NT])
        Zs = sb("Zs", [P, NT])
        Ts = sb("Ts", [P, NT])
        th = sb("th", [P, NT])
        Ms = sb("Ms", [P, NT])
        cs = sb("cs", [P, NT])
        fs = sb("fs", [P, NT])
        Zk = sb("Zk", [P, NT])
        rz = sb("rz", [P, NT])
        arena = sb("arena", [P, 34816])
        at = [0]

        def view(words):
            v = arena[:, at[0]:at[0] + words]
            at[0] += words
            return v

        h2 = view(NT * (D + 2)).rearrange("p (t d) -> p t d", t=NT)
        a2bc = view(N)
        adjn = view(3 * N).rearrange("p (s n) -> p s n", s=3)
        att = view(2 * N).rearrange("p (s n) -> p s n", s=2)
        att2 = view(2 * N).rearrange("p (s n) -> p s n", s=2)
        adjT = view(2 * N).rearrange("p (s n) -> p s n", s=2)
        attT = view(2 * N).rearrange("p (s n) -> p s n", s=2)
        colacc = view(N)
        wrb = view(KD * P).rearrange("p (c n) -> p c n", c=KD)
        albc = view(2 * D).rearrange("p (s n) -> p s n", s=2)
        wjunk = view(D)
        We = view(KD * (D + 2)).rearrange("p (c n) -> p c n", c=KD)
        tA = view(2 * D).rearrange("p (s n) -> p s n", s=2)
        tB = view(2 * D).rearrange("p (s n) -> p s n", s=2)
        at[0] = 0
        V = view(NT * 2 * D).rearrange("p (t d) -> p t d", t=NT)
        V3 = view(NT * D).rearrange("p (t d) -> p t d", t=NT)
        GT = view(N)[0:DA, :]
        KT = view(N)[0:DA, :]
        E = view(SLOTS * N).rearrange("p (s n) -> p s n", s=SLOTS)
        AT = view(2 * N).rearrange("p (s n) -> p s n", s=2)
        ST = view(2 * N).rearrange("p (s n) -> p s n", s=2)
        nat = view(2 * D).rearrange("p (s n) -> p s n", s=2)
        natT = view(2 * D).rearrange("p (s n) -> p s n", s=2)
        yA = view(2 * 2 * D).rearrange("p (s n) -> p s n", s=2)
        x1r = arena[:, 0:NT * D]

        junk = ctx.enter_context(nc.sbuf_tensor("junk", [P, 2, N], mybir.dt.uint8))
        Lp = ctx.enter_context(nc.psum_tensor("Lp", [P, NQ, BANK], f32))
        pr = ctx.enter_context(nc.psum_tensor("pr", [P, 2, BANK], f32))
        tr = ctx.enter_context(nc.psum_tensor("tr", [P, 2, BANK], f32))

        x_in, w0_in, w1_in, x1_out, x1_in = map(sem, "x_in w0_in w1_in x1_out x1_in".split())
        y_out = sem("y_out")
        adj_in = [sem(f"adj_in{i}") for i in range(3)]
        adjT_out = [sem(f"adjT_out{i}") for i in range(2)]
        st_in = [sem(f"st_in{i}") for i in range(2)]
        consts_set = sem("consts_set")
        var_set = sem("var_set")
        sqrt_set = sem("sqrt_set")
        norm_set = sem("norm_set")
        h_set = sem("h_set")
        wl_set = sem("wl_set")
        nm_set = sem("nm_set")
        exp_set = sem("exp_set")
        att_set = sem("att_set")
        attT_set = sem("attT_set")
        rsum_set = sem("rsum_set")
        colacc_set = sem("colacc_set")
        adjq_full, adjq_free = sem("adjq_full"), sem("adjq_free")
        attq_full, attq_free = sem("attq_full"), sem("attq_free")
        tr_full, tr_free = sem("tr_full"), sem("tr_free")
        pr_full, pr_free = sem("pr_full"), sem("pr_free")
        l_full, l_free = sem("l_full"), sem("l_free")
        max_set = sem("max_set")
        keep_set = sem("keep_set")
        rz_set = sem("rz_set")
        ym_set, ee_set, x1_set = sem("ym_set"), sem("ee_set"), sem("x1_set")
        nat_set = sem("nat_set")
        y_set = sem("y_set")
        inv_set = sem("inv_set")
        fin_set = sem("fin_set")
        xb_set = sem("xb_set")
        out_set = sem("out_set")
        vec_done, act_done, pool_done = sem("vec_done"), sem("act_done"), sem("pool_done")

        TR_H = 0
        TR_W1 = TR_H + NT // 2
        TR_X = TR_W1 + 1
        PR_W12 = 0
        PR_H2 = PR_W12 + 1
        PR_A2 = PR_H2 + NT
        PR_Y = PR_A2 + NQ
        PR_CS = PR_Y + NT
        PR_GK = PR_CS + 1
        uses = {"logits": (0, 0, 0), "flip": (4, 0, 0), "mix": (1, 2, 1), "spread": (1, 3, 1), "second": (0, 1, 1)}
        TRU, PRU, YU = {}, {}, {}
        ntr, npr, ny = TR_X + NT // 2, PR_GK, 0
        GKU = []
        for step in range(2):
            GKU.append(npr)
            npr += 2 * NQ
            for kind, t in ORDER[step]:
                key = (step, kind, t)
                TRU[key], PRU[key], YU[key] = ntr, npr, ny
                a, b, c = uses[kind] if (step == 0 or kind != "mix") else (0, 1, 1)
                ntr, npr, ny = ntr + a, npr + b, ny + c
        NTR, NPR, NY = ntr, npr, ny
        y_parts = [(s, k, t) for s in range(2) for k, t in ORDER[s] if k in ("mix", "spread", "second")]
        panels = [(k, t) for k, t in ORDER[0] if k in ("spread", "second")]

        block = ctx.enter_context(nc.Block())

        @block.sync
        def _(sp):
            sp.dma_start(Xb[:], rows(x)).then_inc(x_in, 16)
            sp.dma_start(We[:, :, 0:D], rows(W)).then_inc(w0_in, 16)
            for i, a in enumerate((attn_l, attn_r)):
                sp.dma_start(albc[:, i, :],
                             a.rearrange("d o -> o d").to_broadcast([P, D])).then_inc(w0_in, 16)

            def load_adj(t):
                if t >= 3:
                    u = t - 2
                    sp.wait_ge(att_set, u)
                    sp.wait_ge(rsum_set, u)
                    sp.wait_ge(colacc_set, u)
                    sp.wait_ge(adjq_full, 4 * u)
                sp.dma_start(adjn[:, t % 3, :], adj[t * P:(t + 1) * P, :]).then_inc(adj_in[t % 3], 16)

            load_adj(0)
            sp.dma_start(W1s[:], rows(W1)).then_inc(w1_in, 16)
            sp.dma_start(W2s[:], W2).then_inc(w1_in, 16)
            sp.dma_start(W3s[:], rows(W3)).then_inc(w1_in, 16)
            for s in range(2):
                sp.dma_start(U12s[:, :, s, 0:D], rows(U1[s])).then_inc(w1_in, 16)
                sp.dma_start(U12s[:, :, s, D:2 * D], rows(U2[s])).then_inc(w1_in, 16)
                sp.dma_start(U3s[:, :, s * D:(s + 1) * D], rows(U3[s])).then_inc(w1_in, 16)
            sp.dma_start(gam[:], gamma.rearrange("(o d) -> o d", o=1).to_broadcast([P, D])).then_inc(w1_in, 16)
            sp.dma_start(bet[:], beta.rearrange("(o d) -> o d", o=1).to_broadcast([P, D])).then_inc(w1_in, 16)
            load_adj(1)
            load_adj(2)
            for t in range(NT):
                sp.wait_ge(adjq_free, 4 * (t + 1))
                sp.dma_start(adjT_dram[t], adjT[:, t % 2, :]).then_inc(adjT_out[t % 2], 16)
                if t + 3 < NT:
                    load_adj(t + 3)
            sp.wait_ge(x1_set, NT)
            sp.dma_start(x1_dram, Xb[:].rearrange("p t d -> p (t d)")).then_inc(x1_out, 16)
            for s in range(2):
                sp.wait_ge(adjT_out[s], 16 * NT // 2)
            sp.wait_ge(h_set, 2 * NT)
            sp.wait_ge(pr_free, PR_CS + 1)
            for n, (kind, t) in enumerate(panels):
                if n >= 2:
                    sp.wait_ge(pr_full, PRU[(0,) + panels[n - 2]] + 1)
                sp.dma_start(ST[:, n % 2, :], adjT_dram[t]).then_inc(st_in[n % 2], 16)
            sp.wait_ge(pr_full, PRU[(0,) + panels[-1]] + 1)
            sp.wait_ge(x1_out, 16)
            sp.dma_start(x1r, x1_dram).then_inc(x1_in, 16)
            for g in range(4):
                sp.wait_ge(out_set, 4 * g + 4)
                sp.dma_start(rows(out)[:, 4 * g:4 * g + 4, :], Xb[:, 4 * g:4 * g + 4, :]).then_inc(y_out, 16)
            sp.wait_ge(y_out, 64)

        @block.gpsimd
        def _(pool):
            done = Tally(pool_done)
            n = done.on(nc.gpsimd.memset(ident[:], 0.0))
            nc.gpsimd.memset(ones[:], 1.0).then_inc(consts_set, 1)
            pool.wait_ge(pool_done, n)
            nc.gpsimd.affine_select(out=ident[:], in_=ident[:], compare_op=ALU.not_equal, fill=1.0, base=0,
                                    pattern=[[-1, P]], channel_multiplier=1).then_inc(consts_set, 1)
            for t in range(NT):
                pool.wait_ge(adj_in[t % 3], 16 * (t // 3 + 1))
                if t == 0:
                    nc.gpsimd.tensor_copy(colacc[:], adjn[:, 0, :]).then_inc(colacc_set, 1)
                else:
                    pool.wait_ge(colacc_set, t)
                    nc.gpsimd.tensor_tensor(out=colacc[:], in0=colacc[:], in1=adjn[:, t % 3, :],
                                            op=ALU.add).then_inc(colacc_set, 1)
            pool.wait_ge(x1_out, 16)
            pool.wait_ge(h_set, 2 * NT)
            n = done.on(nc.gpsimd.tensor_copy(Xb[:], Xn[:]))
            for m, (s, kind, t) in enumerate(y_parts):
                pool.wait_ge(pool_done, n)
                last_use = 1 if (s, kind) == (0, "mix") or kind == "spread" else 0
                pool.wait_ge(pr_free, PRU[(s, kind, t)] + last_use + 1)
                halves = 1 if kind == "mix" else 2
                for i in range(halves):
                    add = nc.gpsimd.tensor_tensor(out=Xb[:, t, :], in0=Xb[:, t, :],
                                                  in1=yA[:, m % 2, i * D:(i + 1) * D], op=ALU.add)
                    if i < halves - 1:
                        n = done.on(add)
                        pool.wait_ge(pool_done, n)
                add.then_inc(y_set, 1)
                if m + 1 < len(y_parts):
                    pool.wait_ge(y_set, m + 1)
            pool.wait_ge(x1_in, 16)
            for t in range(NT):
                nc.gpsimd.tensor_tensor(out=x1r[:, t * D:(t + 1) * D], in0=x1r[:, t * D:(t + 1) * D],
                                        in1=bet[:], op=ALU.add).then_inc(xb_set, 1)

        @block.scalar
        def _(act):
            def copy(out_, in_, scale=1.0):
                return nc.scalar.activation(out_, in_, ACT.Copy, scale=scale)

            def normalised(first):
                act.wait_ge(var_set, first + 1)
                nc.scalar.activation(sd[:], ve[:], ACT.Sqrt).then_inc(sqrt_set, 1)
                act.wait_ge(norm_set, first + 1)
                if first:
                    act.wait_ge(pr_full, PR_CS)
                for t in range(NT):
                    nc.scalar.activation(Xn[:, t, :], Xb[:, t, :], ACT.Relu, bias=nmr[:, t:t + 1],
                                         scale=rstd[:, t:t + 1]).then_inc(h_set, 1)

            def flipped(base):
                for q in range(NT // 2):
                    n = base + q
                    act.wait_ge(tr_full, n + 1)
                    copy(XT[:, :, q * 2 * P:(q + 1) * 2 * P],
                         tr[:, n % 2, :].rearrange("p (c n) -> p c n", c=KD)).then_inc(tr_free, 1)

            act.wait_ge(x_in, 16)
            normalised(0)
            flipped(TR_H)
            act.wait_ge(tr_full, TR_W1 + 1)
            copy(W1T[:], tr[0:DA, TR_W1 % 2, 0:D]).then_inc(tr_free, 1)
            act.wait_ge(pr_full, PR_W12 + 1)
            copy(W12[:], pr[:, PR_W12 % 2, 0:KD * DA].rearrange("p (c n) -> p c n", c=KD)).then_inc(pr_free, 1)
            for t in range(NT):
                n = PR_H2 + t
                act.wait_ge(pr_full, n + 1)
                copy(h2[:, t, :], pr[:, n % 2, 0:D + 2]).then_inc(pr_free, 1)
            for q in range(NQ):
                n = PR_A2 + q
                act.wait_ge(pr_full, n + 1)
                copy(a2bc[:, q * BANK:(q + 1) * BANK], pr[:, n % 2, :]).then_inc(pr_free, 1)

            def weights(t):
                if t >= 2:
                    act.wait_ge(attq_full, 4 * (t - 1))
                if t == 0:
                    act.wait_ge(pr_free, PR_Y)
                    act.wait_ge(nm_set, 1)
                nc.scalar.activation(att[:, t % 2, :], a2bc[:], ACT.Exp, bias=off1[:, t:t + 1])
                nc.scalar.activation(att2[:, t % 2, :], a2bc[:], ACT.Exp, bias=off2[:, t:t + 1],
                                     scale=ALPHA).then_inc(exp_set, 1)
                act.wait_ge(adj_in[t % 3], 16 * (t // 3 + 1))
                if t >= 2:
                    act.wait_ge(rsum_set, t - 1)
                nc.scalar.activation(junk[:, t % 2, :], adjn[:, t % 3, :], ACT.Copy,
                                     accum_out=rsum[:, t:t + 1]).then_inc(rsum_set, 1)

            def elu_exp(t):
                act.wait_ge(ym_set, t + 1)
                nc.scalar.activation(tA[:, t % 2, :], tA[:, t % 2, :], ACT.Exp).then_inc(ee_set, 1)

            weights(0)
            for t in range(NT):
                if t + 1 < NT:
                    weights(t + 1)
                for q in range(4):
                    n = 4 * t + q
                    act.wait_ge(adjq_full, n + 1)
                    if t >= 2 and q == 0:
                        act.wait_ge(adjT_out[t % 2], 16 * (t // 2))
                    copy(adjT[:, t % 2, q * BANK:(q + 1) * BANK], Lp[:, n % 2, :]).then_inc(adjq_free, 1)
                if t >= 2:
                    elu_exp(t - 2)
            elu_exp(NT - 2)
            elu_exp(NT - 1)
            act.wait_ge(pr_full, PR_CS + 1)
            copy(csum[:], pr[:, PR_CS % 2, 0:NT]).then_inc(pr_free, 1)

            normalised(1)
            flipped(TR_X)
            uses_nat = [0]
            for step in range(2):
                for i in range(2 * NQ):
                    n = GKU[step] + i
                    q = i // 2
                    act.wait_ge(pr_full, n + 1)
                    if step == 0 and i == 0:
                        act.wait_ge(colacc_set, NT)
                        for slot in range(2):
                            act.wait_ge(adjT_out[slot], 16 * NT // 2)
                    copy((GT, KT)[i % 2][:, q * BANK:(q + 1) * BANK], pr[0:DA, n % 2, :]).then_inc(pr_free, 1)
                for kind, t in ORDER[step]:
                    key = (step, kind, t)
                    u, v, m = TRU[key], PRU[key], YU[key]
                    g = step * NT + t
                    if kind == "logits":
                        act.wait_ge(l_full, g + 1)
                        act.wait_ge(max_set, g + 1)
                        nc.scalar.activation(E[:, t % SLOTS, :], Lp[:].rearrange("p q n -> p (q n)"), ACT.Exp,
                                             bias=nmax[:, t:t + 1],
                                             accum_out=Zs[:, t:t + 1]).then_inc(l_free, 1)
                    if kind == "flip":
                        for q in range(4):
                            act.wait_ge(tr_full, u + q + 1)
                            copy(AT[:, t % 2, q * BANK:(q + 1) * BANK], tr[:, (u + q) % 2, :]).then_inc(tr_free, 1)
                    if kind in ("mix", "spread") and not (kind == "mix" and step == 1):
                        k = uses_nat[0]
                        uses_nat[0] += 1
                        act.wait_ge(pr_full, v + 1)
                        if kind == "mix":
                            act.wait_ge(rz_set, g // 2 + 1)
                        copy(nat[:, k % 2, :], pr[:, v % 2, 0:D],
                             rz[:, t:t + 1] if kind == "mix" else 1.0).then_inc(pr_free, 1)
                        act.wait_ge(tr_full, u + 1)
                        where = XT[:, :, t * P:(t + 1) * P] if kind == "mix" else \
                            natT[:, k % 2, :].rearrange("p (c n) -> p c n", c=KD)
                        copy(where, tr[:, u % 2, 0:D].rearrange("p (c n) -> p c n", c=KD)).then_inc(tr_free, 1)
                    if kind in ("mix", "spread", "second") and m >= 2:
                        act.wait_ge(y_set, m - 1)
                    if kind == "mix" and step == 0:
                        act.wait_ge(pr_full, v + 2)
                        copy(yA[:, m % 2, 0:D], pr[:, (v + 1) % 2, 0:D])
                        copy(V3[:, t, :], pr[:, (v + 1) % 2, D:2 * D]).then_inc(pr_free, 1)
                    if kind == "mix" and step == 1:
                        act.wait_ge(pr_full, v + 1)
                        act.wait_ge(rz_set, g // 2 + 1)
                        nc.scalar.activation(yA[:, m % 2, 0:D], pr[:, v % 2, 0:D], ACT.Copy,
                                             scale=rz[:, t:t + 1]).then_inc(pr_free, 1)
                    if kind == "spread":
                        act.wait_ge(pr_full, v + 2)
                        if t == 0:
                            act.wait_ge(inv_set, 1)
                        b = pr[:, (v + 1) % 2, :]
                        copy(yA[:, m % 2, 0:D], b[:, 0:D], rinv[:, t:t + 1])
                        copy(yA[:, m % 2, D:2 * D], b[:, D:2 * D],
                             cinv[:, t:t + 1]).then_inc(pr_free, 1)
                        act.wait_ge(pr_full, v + 3)
                        b = pr[:, (v + 2) % 2, :]
                        copy(V[:, t, 0:D], b[:, 0:D], rinv[:, t:t + 1])
                        copy(V[:, t, D:2 * D], b[:, D:2 * D], cinv[:, t:t + 1]).then_inc(pr_free, 1)
                    if kind == "second":
                        act.wait_ge(pr_full, v + 1)
                        b = pr[:, v % 2, :]
                        copy(yA[:, m % 2, 0:D], b[:, 0:D], rinv[:, t:t + 1])
                        copy(yA[:, m % 2, D:2 * D], b[:, D:2 * D],
                             cinv[:, t:t + 1]).then_inc(pr_free, 1)
            act.wait_ge(var_set, 3)
            nc.scalar.activation(sd[:], ve[:], ACT.Sqrt).then_inc(sqrt_set, 1)
            act.wait_ge(norm_set, 3)
            for t in range(NT):
                nc.scalar.activation(Xn[:, t, :], Xb[:, t, :], ACT.Identity, bias=nmr[:, t:t + 1],
                                     scale=rstd[:, t:t + 1]).then_inc(fin_set, 1)

        @block.tensor
        def _(pe):
            pe.wait_ge(consts_set, 2)

            def ring(free, n, depth=2):
                if n >= depth:
                    pe.wait_ge(free, n - depth + 1)

            def flip_rows(base, h_base):
                for q in range(NT // 2):
                    n = base + q
                    pe.wait_ge(h_set, h_base + 2 * q + 2)
                    ring(tr_free, n)
                    for i in range(2):
                        for c in range(KD):
                            last = nc.tensor.transpose(tr[:, n % 2, (2 * c + i) * P:(2 * c + i + 1) * P],
                                                       Xn[:, 2 * q + i, c * P:(c + 1) * P], ident[:])
                    last.then_inc(tr_full, 1)

            flip_rows(TR_H, 0)
            pe.wait_ge(w1_in, 16 * 11)
            ring(tr_free, TR_W1)
            for c in range(KD):
                last = nc.tensor.transpose(tr[0:DA, TR_W1 % 2, c * P:(c + 1) * P], W1s[:, c, :], ident[:])
            last.then_inc(tr_full, 1)
            pe.wait_ge(tr_free, TR_W1 + 1)
            for c in range(KD):
                last = nc.tensor.matmul(pr[:, PR_W12 % 2, c * DA:(c + 1) * DA], W1T[:, c * P:(c + 1) * P], W2s[:],
                                        start=True, stop=True)
            last.then_inc(pr_full, 1)
            pe.wait_ge(wl_set, 2)
            for t in range(NT):
                n = PR_H2 + t
                ring(pr_free, n)
                for c in range(KD):
                    last = nc.tensor.matmul(pr[:, n % 2, 0:D + 2], XT[:, c, t * P:(t + 1) * P], We[:, c, :],
                                            start=c == 0, stop=c == KD - 1)
                last.then_inc(pr_full, 1)
            pe.wait_ge(wl_set, 3)
            for q in range(NQ):
                n = PR_A2 + q
                ring(pr_free, n)
                for c in range(KD):
                    last = nc.tensor.matmul(pr[:, n % 2, :], wrb[:, c, :], XT[:, c, q * BANK:(q + 1) * BANK],
                                            start=c == 0, stop=c == KD - 1)
                last.then_inc(pr_full, 1)

            def flips(t):
                pe.wait_ge(adj_in[t % 3], 16 * (t // 3 + 1))
                for q in range(4):
                    n = 4 * t + q
                    ring(adjq_free, n)
                    for i in range(4):
                        j = (4 * q + i) * P
                        last = nc.tensor.transpose(Lp[:, n % 2, i * P:(i + 1) * P], adjn[:, t % 3, j:j + P], ident[:])
                    last.then_inc(adjq_full, 1)
                pe.wait_ge(att_set, t + 1)
                for q in range(4):
                    n = 4 * t + q
                    ring(attq_free, n)
                    for i in range(4):
                        j = (4 * q + i) * P
                        last = nc.tensor.transpose(Lp[:, 2 + n % 2, i * P:(i + 1) * P], att[:, t % 2, j:j + P], ident[:])
                    last.then_inc(attq_full, 1)

            def product(n, panel, right, width, own=None):
                ring(pr_free, n)
                for j in range(NT):
                    last = nc.tensor.matmul(pr[:, n % 2, 0:width], panel[:, j * P:(j + 1) * P], right[:, j, 0:width],
                                            start=j == 0, stop=j == NT - 1 and own is None)
                if own is not None:
                    last = nc.tensor.matmul(pr[:, n % 2, 0:width], ident[:], own, start=False, stop=True)
                last.then_inc(pr_full, 1)

            flips(0)
            for t in range(NT):
                if t + 1 < NT:
                    flips(t + 1)
                pe.wait_ge(attq_free, 4 * (t + 1))
                product(PR_Y + t, attT[:, t % 2, :], h2, D)
            pe.wait_ge(colacc_set, NT)
            ring(pr_free, PR_CS)
            for j in range(NT):
                last = nc.tensor.matmul(pr[:, PR_CS % 2, j:j + 1], colacc[:, j * P:(j + 1) * P], ones[:, 0:1],
                                        start=True, stop=True)
            last.then_inc(pr_full, 1)

            flip_rows(TR_X, NT)
            np_ = [0]
            nn = [0]
            for step in range(2):
                last_xt = TR_X + NT // 2 if step == 0 else max(TRU[(0, "mix", t)] for t in range(NT)) + 1
                pe.wait_ge(tr_free, last_xt)
                for q in range(NQ):
                    for i, w in enumerate((W12, W3s)):
                        n = GKU[step] + 2 * q + i
                        ring(pr_free, n)
                        for c in range(KD):
                            last = nc.tensor.matmul(pr[0:DA, n % 2, :], w[:, c, :], XT[:, c, q * BANK:(q + 1) * BANK],
                                                    start=c == 0, stop=c == KD - 1)
                        last.then_inc(pr_full, 1)
                pe.wait_ge(pr_free, GKU[step] + 2 * NQ)
                for kind, t in ORDER[step]:
                    key = (step, kind, t)
                    u, v = TRU[key], PRU[key]
                    g = step * NT + t
                    if kind == "logits":
                        if g:
                            pe.wait_ge(l_free, g)
                        for q in range(NQ):
                            last = nc.tensor.matmul(Lp[:, q, :], GT[:, t * P:(t + 1) * P], KT[:, q * BANK:(q + 1) * BANK],
                                                    start=True, stop=True)
                        last.then_inc(l_full, 1)
                    if kind == "flip":
                        pe.wait_ge(keep_set, g + 1)
                        for q in range(4):
                            ring(tr_free, u + q)
                            for i in range(4):
                                j = (4 * q + i) * P
                                last = nc.tensor.transpose(tr[:, (u + q) % 2, i * P:(i + 1) * P],
                                                           E[:, t % SLOTS, j:j + P], ident[:])
                            last.then_inc(tr_full, 1)
                    if kind == "mix":
                        pe.wait_ge(tr_free, TRU[(step, "flip", t)] + 4)
                        product(v, AT[:, t % 2, :], V3 if step else Xn, D)
                    if kind == "spread":
                        pe.wait_ge(st_in[np_[0] % 2], 16 * (np_[0] // 2 + 1))
                        product(v, ST[:, np_[0] % 2, :], Xn, D, own=Xn[:, t, :])
                        np_[0] += 1
                    if kind == "second":
                        pe.wait_ge(pr_free, PRU[(0, "spread", NT - 1)] + 3)
                        pe.wait_ge(st_in[np_[0] % 2], 16 * (np_[0] // 2 + 1))
                        product(v, ST[:, np_[0] % 2, :], V, 2 * D, own=V[:, t, :])
                        np_[0] += 1
                    if kind == "spread" or (kind == "mix" and step == 0):
                        k = nn[0]
                        nn[0] += 1
                        pe.wait_ge(pr_free, v + 1)
                        ring(tr_free, u)
                        for c in range(KD):
                            last = nc.tensor.transpose(tr[:, u % 2, c * P:(c + 1) * P], nat[:, k % 2, c * P:(c + 1) * P],
                                                       ident[:])
                        last.then_inc(tr_full, 1)
                        pe.wait_ge(tr_free, u + 1)
                        for s in range(1 if kind == "mix" else 2):
                            ring(pr_free, v + 1 + s)
                            for c in range(KD):
                                if kind == "mix":
                                    left, right = XT[:, c, t * P:(t + 1) * P], U3s[:, c, :]
                                else:
                                    left, right = natT[:, k % 2, c * P:(c + 1) * P], U12s[:, c, s, :]
                                last = nc.tensor.matmul(pr[:, (v + 1 + s) % 2, :], left, right,
                                                        start=c == 0, stop=c == KD - 1)
                            last.then_inc(pr_full, 1)

        @block.vector
        def _(dve):
            done = Tally(vec_done)

            def link(ins):
                done.on(ins)
                dve.wait_ge(vec_done, done.n)

            def stats(t):
                link(nc.vector.bn_stats(st6[:, t, :], Xb[:, t, :]))
                return nc.vector.bn_aggr(mv[:, t, :], st6[:, t, :])

            def scales(n):
                nc.vector.tensor_scalar(out=ve[:], in0=mv[:, :, 1], scalar1=EPS_LN, scalar2=None,
                                        op0=ALU.add).then_inc(var_set, 1)
                dve.wait_ge(sqrt_set, n)
                link(nc.vector.reciprocal(y0[:], sd[:]))
                link(nc.vector.tensor_tensor(out=yt[:], in0=y0[:], in1=y0[:], op=ALU.mult))
                link(nc.vector.tensor_tensor(out=yt[:], in0=yt[:], in1=ve[:], op=ALU.mult))
                link(nc.vector.tensor_scalar(out=yt[:], in0=yt[:], scalar1=-0.5, scalar2=1.5,
                                             op0=ALU.mult, op1=ALU.add))
                link(nc.vector.tensor_tensor(out=rstd[:], in0=y0[:], in1=yt[:], op=ALU.mult))
                nc.vector.scalar_tensor_tensor(out=nmr[:], in0=mv[:, :, 0], scalar=-1.0, in1=rstd[:],
                                               op0=ALU.mult, op1=ALU.mult).then_inc(norm_set, 1)

            dve.wait_ge(x_in, 16)
            for t in range(NT):
                link(stats(t))
            scales(1)
            dve.wait_ge(w0_in, 48)
            for i in range(2):
                for c in range(KD):
                    link(nc.vector.scalar_tensor_tensor(out=wjunk[:], in0=We[:, c, 0:D], scalar=1.0,
                                                        in1=albc[:, i, :], op0=ALU.mult, op1=ALU.mult,
                                                        accum_out=We[:, c, D + i:D + i + 1]))
            nc.vector.memset(wrb[:], 1.0).then_inc(wl_set, 2)
            dve.wait_ge(wl_set, 2)
            for c in range(KD):
                last = nc.vector.tensor_scalar(out=wrb[:, c, :], in0=wrb[:, c, :], scalar1=We[:, c, D + 1:D + 2],
                                               scalar2=None, op0=ALU.mult)
            last.then_inc(wl_set, 1)
            dve.wait_ge(pr_free, PR_Y)
            link(nc.vector.reduce_max(a2max[:], a2bc[:], axis=AX))
            link(nc.vector.tensor_scalar(out=sm[:], in0=h2[:, :, D], scalar1=a2max[:], scalar2=None, op0=ALU.add))
            link(nc.vector.tensor_scalar(out=sm2[:], in0=sm[:], scalar1=ALPHA, scalar2=None, op0=ALU.mult))
            link(nc.vector.tensor_tensor(out=sm[:], in0=sm[:], in1=sm2[:], op=ALU.max))
            done.on(nc.vector.tensor_tensor(out=off1[:], in0=h2[:, :, D], in1=sm[:], op=ALU.subtract))
            nc.vector.scalar_tensor_tensor(out=off2[:], in0=h2[:, :, D], scalar=ALPHA, in1=sm[:], op0=ALU.mult,
                                           op1=ALU.subtract).then_inc(nm_set, 1)

            def elu_parts(t):
                n = PR_Y + t
                dve.wait_ge(pr_full, n + 1)
                if t >= 2:
                    dve.wait_ge(ee_set, t - 1)
                nc.vector.tensor_scalar(out=tA[:, t % 2, :], in0=pr[:, n % 2, 0:D], scalar1=rden[:, t:t + 1],
                                        scalar2=0.0, op0=ALU.mult, op1=ALU.min).then_inc(ym_set, 1)
                nc.vector.tensor_scalar(out=tB[:, t % 2, :], in0=pr[:, n % 2, 0:D], scalar1=rden[:, t:t + 1],
                                        scalar2=0.0, op0=ALU.mult, op1=ALU.max).then_inc(pr_free, 1)

            def residual(t):
                dve.wait_ge(ee_set, t + 1)
                dve.wait_ge(pr_free, PR_Y + t + 1)
                link(nc.vector.scalar_tensor_tensor(out=tB[:, t % 2, :], in0=tA[:, t % 2, :], scalar=-1.0,
                                                    in1=tB[:, t % 2, :], op0=ALU.add, op1=ALU.add))
                nc.vector.tensor_tensor(out=Xb[:, t, :], in0=Xb[:, t, :], in1=tB[:, t % 2, :],
                                        op=ALU.add).then_inc(x1_set, 1)
                dve.wait_ge(x1_set, t + 1)
                link(stats(t))

            for t in range(NT + 3):
                if t < NT:
                    a = att[:, t % 2, :]
                    dve.wait_ge(exp_set, t + 1)
                    dve.wait_ge(adj_in[t % 3], 16 * (t // 3 + 1))
                    link(nc.vector.tensor_tensor(out=a, in0=a, in1=att2[:, t % 2, :], op=ALU.max))
                    nc.vector.scalar_tensor_tensor(out=a, in0=a, scalar=1.0, in1=adjn[:, t % 3, :], op0=ALU.mult,
                                                   op1=ALU.mult, accum_out=deno[:, t:t + 1]).then_inc(att_set, 1)
                    dve.wait_ge(att_set, t + 1)
                    link(nc.vector.tensor_scalar(out=rden[:, t:t + 1], in0=deno[:, t:t + 1], scalar1=EPS_ATT,
                                                 scalar2=None, op0=ALU.add))
                    done.on(nc.vector.reciprocal(rden[:, t:t + 1], rden[:, t:t + 1]))
                    for q in range(4):
                        n = 4 * t + q
                        dve.wait_ge(attq_full, n + 1)
                        if t >= 2 and q == 0:
                            dve.wait_ge(pr_full, PR_Y + t - 1)
                        nc.vector.tensor_copy(attT[:, t % 2, q * BANK:(q + 1) * BANK],
                                              Lp[:, 2 + n % 2, :]).then_inc(attq_free, 1)
                if 2 <= t < NT + 2:
                    elu_parts(t - 2)
                if t >= 3:
                    residual(t - 3)
            scales(2)
            dve.wait_ge(pr_free, PR_CS + 1)
            dve.wait_ge(rsum_set, NT)
            for total, inverse in ((rsum, rinv), (csum, cinv)):
                link(nc.vector.tensor_scalar(out=inverse[:], in0=total[:], scalar1=1.0, scalar2=1e-12,
                                             op0=ALU.add, op1=ALU.max))
                last = nc.vector.reciprocal(inverse[:], inverse[:])
            last.then_inc(inv_set, 1)

            for step in range(2):
                pending = []

                def control(q, k):
                    two = slice(2 * q, 2 * q + 2)
                    up = RATIO[k + 1] if k + 1 < STEPS else 1.0
                    down = up / RATIO[k]

                    def compare():
                        dve.wait_ge(vec_done, probed[q])
                        compared[q] = done.on(nc.vector.tensor_tensor(out=cs[:, two], in0=Ms[:, two], in1=Ts[:, two],
                                                                      op=ALU.is_ge))

                    def factor():
                        dve.wait_ge(vec_done, compared[q])
                        compared[q] = done.on(nc.vector.tensor_scalar(out=fs[:, two], in0=cs[:, two],
                                                                      scalar1=up - down, scalar2=down,
                                                                      op0=ALU.mult, op1=ALU.add))

                    def move():
                        dve.wait_ge(vec_done, compared[q])
                        moved[q] = done.on(nc.vector.tensor_tensor(out=th[:, two], in0=th[:, two], in1=fs[:, two],
                                                                   op=ALU.mult))
                    return [compare, factor, move]

                probed, compared, moved = {}, {}, {}
                junk_free = [done.n, done.n]
                for unit in search_units():
                    kind, i = unit[0], unit[1]
                    if kind == "max":
                        g = step * NT + i
                        dve.wait_ge(l_full, g + 1)
                        nc.vector.reduce_max(nmax[:, i:i + 1], Lp[:].rearrange("p q n -> p (q n)"), axis=AX,
                                             negate=True).then_inc(max_set, 1)
                    if kind == "begin":
                        two = slice(2 * i, 2 * i + 2)
                        dve.wait_ge(l_free, step * NT + 2 * i + 2)
                        done.on(nc.vector.tensor_scalar(out=Ts[:, two], in0=Zs[:, two], scalar1=P_NUC, scalar2=None,
                                                        op0=ALU.mult))
                        moved[i] = done.on(nc.vector.tensor_scalar(out=th[:, two], in0=Zs[:, two],
                                                                   scalar1=LOW_END * RATIO[0], scalar2=None,
                                                                   op0=ALU.mult))
                    if kind == "probe":
                        k = unit[2]
                        if pending and pending[0] == i:
                            for f in pending[1]:
                                f()
                            pending = []
                        dve.wait_ge(vec_done, moved[i])
                        for t in (2 * i, 2 * i + 1):
                            e = E[:, t % SLOTS, :]
                            dve.wait_ge(vec_done, junk_free[t % 2])
                            probed[i] = junk_free[t % 2] = done.on(nc.vector.scalar_tensor_tensor(
                                out=junk[:, t % 2, :], in0=e, scalar=th[:, t:t + 1], in1=e, op0=ALU.is_gt, op1=ALU.mult,
                                accum_out=Ms[:, t:t + 1]))
                            if pending and t % 2 == 0:
                                pending[1].pop(0)()
                        if pending:
                            for f in pending[1]:
                                f()
                        pending = [i, control(i, k)]
                    if kind == "keep":
                        if pending and pending[0] == i:
                            for f in pending[1]:
                                f()
                            pending = []
                        dve.wait_ge(vec_done, moved[i])
                        for t in (2 * i, 2 * i + 1):
                            e = E[:, t % SLOTS, :]
                            nc.vector.scalar_tensor_tensor(out=e, in0=e, scalar=th[:, t:t + 1], in1=e, op0=ALU.is_gt,
                                                           op1=ALU.mult, accum_out=Zk[:, t:t + 1]).then_inc(keep_set, 1)
                        dve.wait_ge(keep_set, step * NT + 2 * i + 2)
                        nc.vector.reciprocal(rz[:, 2 * i:2 * i + 2], Zk[:, 2 * i:2 * i + 2]).then_inc(rz_set, 1)
            for t in range(NT):
                dve.wait_ge(y_set, YU[(1, "mix", t)] + 1)
                link(stats(t))
            scales(3)
            for t in range(NT):
                dve.wait_ge(fin_set, t + 1)
                link(nc.vector.tensor_tensor(out=Xn[:, t, :], in0=Xn[:, t, :], in1=gam[:], op=ALU.mult))
                dve.wait_ge(xb_set, t + 1)
                nc.vector.tensor_tensor(out=Xb[:, t, :], in0=Xn[:, t, :], in1=x1r[:, t * D:(t + 1) * D],
                                        op=ALU.add).then_inc(out_set, 1)


_INS = ["x", "adj", "L0_gnn_W", "L0_gnn_attn_l", "L0_gnn_attn_r", "L1_gnn_W1", "L1_gnn_W2", "L1_gnn_W3",
        "L1_gnn_U1", "L1_gnn_U2", "L1_gnn_U3", "L1_gnn_gamma", "L1_gnn_beta"]


def kernel(**inputs):
    import numpy as np
    import concourse.bacc as bacc
    from concourse.bass_utils import run_bass_kernel_spmd

    nc = bacc.Bacc("TRN2", target_bir_lowering=False, num_devices=1)
    arrays, args = {}, []
    for name in _INS:
        a = np.ascontiguousarray(inputs[name])
        arrays[f"in_{name}"] = a
        args.append(nc.dram_tensor(f"in_{name}", a.shape, mybir.dt.from_np(a.dtype), kind="ExternalInput").ap())
    out = nc.dram_tensor("out", (N, D), mybir.dt.float32, kind="ExternalOutput").ap()
    build(nc, *args, out)
    r = run_bass_kernel_spmd(nc, [arrays], core_ids=[0])
    return r.results[0]["out"]
```

```python
import concourse.bass as bass
import concourse.mybir as mybir
from concourse.alu_op_type import AluOpType as ALU

N = 2048
D = 256
DA = 64
P = 128
NT = N // P
KD = D // P
BANK = 512
NQ = N // BANK
ALPHA = 0.2
EPS_ATT = 1e-9
EPS_LN = 1e-5
P_NUC = 0.9

LOG2_RANGE = 15.0
STEPS = 20
RATIO = [2.0 ** (LOG2_RANGE / 2 ** (k + 1)) for k in range(STEPS)]
LOW_END = (1 - P_NUC) / N * (1 - 1e-5)
COARSE = (5, 8)
FINE = (9, 12)
LIFTS = (2, 3)
MARGIN = 1 + 1e-6
SLOTS = 4
SEG = 64
NSEG = N // SEG
NC = 8 * NSEG


def staggered(items):
    tasks = []
    for i in range(len(items) + 2):
        for lag, what in enumerate(("", "turn_", "use_")):
            if 0 <= i - lag < len(items):
                kind, t = items[i - lag]
                tasks.append((what + kind, t))
    return tasks


def order_of_step(step):
    side = [("spread" if step == 0 else "second", t) for t in range(NT)]
    tasks = [("gk", q) for q in range(NQ)] if step == 0 else []
    tasks += [("logits", t) for t in range(SLOTS)]
    first, side = side[:SIDE_FIRST[step]], side[SIDE_FIRST[step]:]
    tasks += staggered(first) if step == 0 else first
    for a in range(0, NT, 2):
        tasks += [("flip", a), ("flip", a + 1)]
        logits = [("logits", t + SLOTS) for t in (a, a + 1) if t + SLOTS < NT]
        mixes = [("mix", a), ("mix", a + 1)]
        now, side = side[:2], side[2:]
        tasks += logits[:1]
        if step == 0:
            if a == NT - 2:
                tasks += mixes + [("turn_" + k, t) for k, t in mixes] + [("next_gk", NQ - 1)]
                tasks += [("use_" + k, t) for k, t in mixes]
            else:
                work = staggered(mixes + now)
                tasks += work[:1] + logits[1:] + work[1:]
            if a == NT - 4:
                tasks += [("next_gk", q) for q in range(NQ - 1)]
        else:
            tasks += mixes[:1] + logits[1:] + now[:1] + mixes[1:] + now[1:]
    assert not side
    return tasks


SIDE_FIRST = (4, 3)
ORDER = [order_of_step(0), order_of_step(1)]
def scalar_order(step):
    tasks, lifts = [], []
    for kind, t in ORDER[step]:
        if kind in LIFTS_BEFORE[step]:
            for _ in range(LIFTS_BEFORE[step][kind]):
                if lifts:
                    tasks.append(lifts.pop(0))
                    if lifts and lifts[0][0] == "steer":
                        tasks.append(lifts.pop(0))
        if kind == "flip" and t % 2 == 0:
            tasks += lifts
            lifts = []
        tasks.append((kind, t))
        if kind == "logits" and t % 2 and t > 1:
            q = t // 2
            tasks.append(("lift_from", q))
            for k in range(LIFTS[step]):
                lifts += [("lift", t - 1, k), ("lift", t, k), ("steer", q, k)]
    return tasks


MAX_AFTER = ((3, 8, 5), (3, 8, 5))
LIFTS_BEFORE = ({"mix": 1, "spread": 1, "use_mix": 1, "use_spread": 1}, {"mix": 1, "second": 4})


def coarse_units(q, coarse, first):
    units = [("begin", q)]
    for k in range(first, coarse):
        units += [("probe", 2 * q, k), ("probe", 2 * q + 1, k)]
        units += [("compare", q, k), ("factor", q, k), ("move", q, k)]
    return units


def search_units(step):
    coarse, lifts = COARSE[step], LIFTS[step]
    pairs = NT // 2
    units = [("max", 0), ("max", 1)]
    ahead = coarse_units(0, coarse, 0)
    units += ahead[:6] + [("max", 2)] + ahead[6:11] + [("max", 3)] + ahead[11:]
    for q in range(pairs):
        units += [("collect", 2 * q)]
        units += [("collect", 2 * q + 1), ("resolve", q)]
        for k in range(coarse, FINE[step]):
            units += [("fine", 2 * q, k), ("fine", 2 * q + 1, k), ("compare", q, k), ("factor", q, k), ("move", q, k)]
        units += [("finish", q)]
        ahead = coarse_units(q + 1, coarse, lifts) if q + 1 < pairs else []
        n = MAX_AFTER[step][0]
        units += ahead[:n] + [("check", q), ("keep", q)]
        ahead = ahead[n:]
        for t in (2 * q + 4, 2 * q + 5):
            n = MAX_AFTER[step][1 + t % 2]
            units += ahead[:n]
            ahead = ahead[n:]
            if t < NT:
                units += [("max", t)]
        units += ahead
    return units


class Tally:

    def __init__(self, sem):
        self.sem, self.n = sem, 0

    def on(self, ins, by=1):
        self.n += by
        ins.then_inc(self.sem, by)
        return self.n


def build(nc, x, adj, W, attn_l, attn_r, W1, W2, W3, U1, U2, U3, gamma, beta, out):
    from contextlib import ExitStack
    f32 = mybir.dt.float32
    ACT = mybir.ActivationFunctionType
    AX = mybir.AxisListType.X

    adjT_dram = nc.dram_tensor("adjT_scratch", [NT, P, NT * P], f32, kind="Internal").ap()
    x1_dram = nc.dram_tensor("x1_scratch", [P, NT * D], f32, kind="Internal").ap()
    rows = lambda ap: ap.rearrange("(t p) d -> p t d", p=P)

    with ExitStack() as ctx:
        def sb(name, shape):
            return ctx.enter_context(nc.sbuf_tensor(name, shape, f32))

        def sem(name):
            return ctx.enter_context(nc.semaphore(name))

        ident = sb("ident", [P, P])
        ones = sb("ones", [P, 2])
        Xn = sb("Xn", [P, NT, D])
        XT = sb("XT", [P, KD, N])
        Xb = sb("Xb", [P, NT, D])
        W12 = sb("W12", [P, KD, 2, DA])
        W3s = sb("W3s", [P, KD, 2, DA])
        U12s = sb("U12s", [P, KD, 2, 2 * D])
        U3s = sb("U3s", [P, KD, 2 * D])
        st6 = sb("st6", [P, NT, 6])
        mv = sb("mv", [P, NT, 2])
        ve = sb("ve", [P, NT])
        sd = sb("sd", [P, NT])
        y0 = sb("y0", [P, NT])
        yt = sb("yt", [P, NT])
        rstd = sb("rstd", [P, NT])
        nmr = sb("nmr", [P, NT])
        a2max = sb("a2max", [P, 1])
        sm = sb("sm", [P, NT])
        sm2 = sb("sm2", [P, NT])
        off1 = sb("off1", [P, NT])
        off2 = sb("off2", [P, NT])
        deno = sb("deno", [P, NT])
        rden = sb("rden", [P, NT])
        rsum = sb("rsum", [P, NT])
        rinv = sb("rinv", [P, NT])
        csum = sb("csum", [P, NT])
        cinv = sb("cinv", [P, NT])
        nmax = sb("nmax", [P, NT])
        Zs = sb("Zs", [P, NT])
        Ts = sb("Ts", [P, NT])
        th = sb("th", [P, NT])
        Ms = sb("Ms", [P, NT])
        cs = sb("cs", [P, NT])
        fs = sb("fs", [P, NT])
        Zk = sb("Zk", [P, NT])
        rz = sb("rz", [P, NT])
        ups = sb("ups", [P, STEPS])
        downs = sb("downs", [P, STEPS])
        mbuf = sb("mbuf", [P, N // 2])
        cand = sb("cand", [P, 2, NC])
        lifted = ctx.enter_context(nc.sbuf_tensor("lifted", [P, 2, N], mybir.dt.uint8))
        tails = sb("tails", [P, 2, NT])
        hi = sb("hi", [P, NT])
        eighth = sb("eighth", [P, NT])
        lost = sb("lost", [P, NT])
        lost_pair = sb("lost_pair", [P, NT])
        lost_any = ctx.enter_context(nc.sbuf_tensor("lost_any", [P, NT], mybir.dt.int32))
        arena = sb("arena", [P, 33792])
        at = [0]

        def view(words):
            v = arena[:, at[0]:at[0] + words]
            at[0] += words
            return v

        h2 = view(NT * (D + 2)).rearrange("p (t d) -> p t d", t=NT)
        a2bc = view(N)
        adjn = view(3 * N).rearrange("p (s n) -> p s n", s=3)
        att = view(2 * N).rearrange("p (s n) -> p s n", s=2)
        att2 = view(2 * N).rearrange("p (s n) -> p s n", s=2)
        adjT = view(2 * N).rearrange("p (s n) -> p s n", s=2)
        attT = view(2 * N).rearrange("p (s n) -> p s n", s=2)
        colacc = view(N)
        wrb = view(KD * P).rearrange("p (c n) -> p c n", c=KD)
        albc = view(2 * D).rearrange("p (s n) -> p s n", s=2)
        wjunk = view(D)
        We = view(KD * (D + 2)).rearrange("p (c n) -> p c n", c=KD)
        tA = view(2 * D).rearrange("p (s n) -> p s n", s=2)
        tB = view(2 * D).rearrange("p (s n) -> p s n", s=2)
        W1s = view(KD * DA).rearrange("p (c n) -> p c n", c=KD)
        W1T = view(D)[0:DA, :]
        W2s = view(DA)[0:DA, :]
        at[0] = 0
        V = view(NT * 2 * D).rearrange("p (t d) -> p t d", t=NT)
        V3 = view(NT * D).rearrange("p (t d) -> p t d", t=NT)
        GT = view(N)
        KT = view(N // 2)
        E = view(SLOTS * N).rearrange("p (s n) -> p s n", s=SLOTS)
        AT = view(2 * N).rearrange("p (s n) -> p s n", s=2)
        ST = view(2 * N).rearrange("p (s n) -> p s n", s=2)
        nat = view(2 * D).rearrange("p (s n) -> p s n", s=2)
        natT = view(2 * D).rearrange("p (s n) -> p s n", s=2)
        yA = view(2 * 2 * D).rearrange("p (s n) -> p s n", s=2)
        x1r = arena[:, 0:NT * D]
        top8, sum2, sum4 = (st6[:].rearrange("p a b -> p (a b)")[:, 32 * i:32 * i + 32].rearrange("p (s n) -> p s n", s=2)
                            for i in range(3))
        cut = yt
        gam = arena[:, NT * D:NT * D + D]
        bet = arena[:, NT * D + D:NT * D + 2 * D]
        nth, aim, above, signs, rest, nlift0, nlift1, side_of = off1, off2, deno, rden, sm, sm2, rsum, csum

        junk = mbuf[:].bitcast(mybir.dt.uint8).rearrange("p (s n) -> p s n", s=2)
        junk2 = ctx.enter_context(nc.sbuf_tensor("junk2", [P, 2, NC], mybir.dt.uint8))
        Lp = ctx.enter_context(nc.psum_tensor("Lp", [P, NQ, BANK], f32))
        pr = ctx.enter_context(nc.psum_tensor("pr", [P, 2, BANK], f32))
        tr = ctx.enter_context(nc.psum_tensor("tr", [P, 2, BANK], f32))

        x_in, w0_in, w1_in, x1_out, x1_in = map(sem, "x_in w0_in w1_in x1_out x1_in".split())
        y_out = sem("y_out")
        adj_in = [sem(f"adj_in{i}") for i in range(3)]
        adjT_out = [sem(f"adjT_out{i}") for i in range(2)]
        st_in = [sem(f"st_in{i}") for i in range(2)]
        consts_set = sem("consts_set")
        var_set = sem("var_set")
        sqrt_set = sem("sqrt_set")
        norm_set = sem("norm_set")
        h_set = sem("h_set")
        wl_set = sem("wl_set")
        nm_set = sem("nm_set")
        exp_set = sem("exp_set")
        att_set = sem("att_set")
        attT_set = sem("attT_set")
        rsum_set = sem("rsum_set")
        colacc_set = sem("colacc_set")
        adjq_full, adjq_free = sem("adjq_full"), sem("adjq_free")
        attq_full, attq_free = sem("attq_full"), sem("attq_free")
        tr_full, tr_free = sem("tr_full"), sem("tr_free")
        pr_full, pr_free = sem("pr_full"), sem("pr_free")
        l_full, l_free = sem("l_full"), sem("l_free")
        max_set = sem("max_set")
        keep_set = sem("keep_set")
        lift_set = sem("lift_set")
        lost_set, any_set = sem("lost_set"), sem("any_set")
        slow_done = sem("slow_done")
        rz_set = sem("rz_set")
        ym_set, ee_set, x1_set = sem("ym_set"), sem("ee_set"), sem("x1_set")
        nat_set = sem("nat_set")
        y_set = sem("y_set")
        inv_set = sem("inv_set")
        fin_set = sem("fin_set")
        xb_set = sem("xb_set")
        out_set = sem("out_set")
        vec_done, act_done, pool_done = sem("vec_done"), sem("act_done"), sem("pool_done")

        TR_H = 0
        TR_W1 = TR_H + NT // 2
        TR_X = TR_W1 + 1
        PR_W12 = 0
        PR_H2 = PR_W12 + 1
        PR_A2 = PR_H2 + NT
        PR_Y = PR_A2 + NQ
        PR_CS = PR_Y + NT
        PR_GK = PR_CS + 1
        Y_KINDS = (("use_mix", "use_spread"), ("mix", "second"))
        uses = {"gk": (0, 2, 0), "next_gk": (0, 2, 0), "logits": (0, 0, 0), "flip": (4, 0, 0), "mix": (0, 1, 0), "turn_mix": (1, 0, 0), "use_mix": (0, 1, 1),
                "spread": (0, 1, 0), "turn_spread": (1, 0, 0), "use_spread": (0, 2, 1), "second": (0, 1, 1)}
        TRU, PRU, YU = {}, {}, {}
        ntr, npr, ny = TR_X + NT // 2, PR_GK, 0
        for step in range(2):
            for kind, t in ORDER[step]:
                key = (step, kind, t)
                TRU[key], PRU[key], YU[key] = ntr, npr, ny
                a, b, c = uses[kind] if (step == 0 or kind != "mix") else (0, 1, 1)
                ntr, npr, ny = ntr + a, npr + b, ny + c
        GK_DONE = [PRU[(0, "gk", NQ - 1)] + 2, PRU[(0, "next_gk", NQ - 1)] + 2]
        items = [(k, t) for k, t in ORDER[0] if k in ("mix", "spread")]
        y_parts = [(s, k, t) for s in range(2) for k, t in ORDER[s] if k in Y_KINDS[s]]
        panels = [(s, k, t) for s in range(2) for k, t in ORDER[s] if k in ("spread", "second")]

        CHECK_BEFORE, seen = [], 0
        for s in range(2):
            for kind, t in ORDER[s]:
                if kind == "flip" and t % 2 == 0:
                    seen = s * NT // 2 + t // 2 + 1
                if kind in Y_KINDS[s]:
                    CHECK_BEFORE.append(seen)

        block = ctx.enter_context(nc.Block())

        @block.sync
        def _(sp):
            sp.dma_start(Xb[:], rows(x)).then_inc(x_in, 16)
            sp.dma_start(We[:, :, 0:D], rows(W)).then_inc(w0_in, 16)
            for i, a in enumerate((attn_l, attn_r)):
                sp.dma_start(albc[:, i, :],
                             a.rearrange("d o -> o d").to_broadcast([P, D])).then_inc(w0_in, 16)

            def load_adj(t):
                if t >= 3:
                    u = t - 2
                    sp.wait_ge(att_set, u)
                    sp.wait_ge(rsum_set, u)
                    sp.wait_ge(colacc_set, u)
                    sp.wait_ge(adjq_full, 4 * u)
                sp.dma_start(adjn[:, t % 3, :], adj[t * P:(t + 1) * P, :]).then_inc(adj_in[t % 3], 16)

            load_adj(0)
            sp.dma_start(W1s[:], rows(W1)).then_inc(w1_in, 16)
            sp.dma_start(W2s[:], W2).then_inc(w1_in, 16)
            for i in range(2):
                sp.dma_start(W3s[:, :, i, :], rows(W3)).then_inc(w1_in, 16)
            for s in range(2):
                sp.dma_start(U12s[:, :, s, 0:D], rows(U1[s])).then_inc(w1_in, 16)
                sp.dma_start(U12s[:, :, s, D:2 * D], rows(U2[s])).then_inc(w1_in, 16)
                sp.dma_start(U3s[:, :, s * D:(s + 1) * D], rows(U3[s])).then_inc(w1_in, 16)
            load_adj(1)
            load_adj(2)
            for t in range(NT):
                sp.wait_ge(adjq_free, 4 * (t + 1))
                sp.dma_start(adjT_dram[t], adjT[:, t % 2, :]).then_inc(adjT_out[t % 2], 16)
                if t + 3 < NT:
                    load_adj(t + 3)
            sp.wait_ge(x1_set, NT)
            sp.dma_start(x1_dram, Xb[:].rearrange("p t d -> p (t d)")).then_inc(x1_out, 16)
            for s in range(2):
                sp.wait_ge(adjT_out[s], 16 * NT // 2)
            sp.wait_ge(h_set, 2 * NT)
            sp.wait_ge(pr_free, PR_CS + 1)
            for n, panel in enumerate(panels):
                if n >= 2:
                    sp.wait_ge(pr_full, PRU[panels[n - 2]] + 1)
                sp.dma_start(ST[:, n % 2, :], adjT_dram[panel[2]]).then_inc(st_in[n % 2], 16)
            sp.wait_ge(pr_full, PRU[panels[-1]] + 1)
            sp.wait_ge(x1_out, 16)
            sp.dma_start(gam, gamma.rearrange("(o d) -> o d", o=1).to_broadcast([P, D])).then_inc(x1_in, 16)
            sp.dma_start(bet, beta.rearrange("(o d) -> o d", o=1).to_broadcast([P, D])).then_inc(x1_in, 16)
            sp.dma_start(x1r, x1_dram).then_inc(x1_in, 16)
            for g in range(4):
                sp.wait_ge(out_set, 4 * g + 4)
                sp.dma_start(rows(out)[:, 4 * g:4 * g + 4, :], Xb[:, 4 * g:4 * g + 4, :]).then_inc(y_out, 16)
            sp.wait_ge(y_out, 64)

        @block.gpsimd
        def _(pool):
            done = Tally(pool_done)
            n = done.on(nc.gpsimd.memset(ident[:], 0.0))
            nc.gpsimd.memset(ones[:], 1.0).then_inc(consts_set, 1)
            pool.wait_ge(pool_done, n)
            nc.gpsimd.affine_select(out=ident[:], in_=ident[:], compare_op=ALU.not_equal, fill=1.0, base=0,
                                    pattern=[[-1, P]], channel_multiplier=1).then_inc(consts_set, 1)
            for t in range(NT):
                pool.wait_ge(adj_in[t % 3], 16 * (t // 3 + 1))
                if t == 0:
                    nc.gpsimd.tensor_copy(colacc[:], adjn[:, 0, :]).then_inc(colacc_set, 1)
                else:
                    pool.wait_ge(colacc_set, t)
                    nc.gpsimd.tensor_tensor(out=colacc[:], in0=colacc[:], in1=adjn[:, t % 3, :],
                                            op=ALU.add).then_inc(colacc_set, 1)
            pool.wait_ge(x1_out, 16)
            pool.wait_ge(h_set, 2 * NT)
            n = done.on(nc.gpsimd.tensor_copy(Xb[:], Xn[:]))
            checks = 0
            for m, (s, kind, t) in enumerate(y_parts):
                while checks < CHECK_BEFORE[m]:
                    pool.wait_ge(lost_set, checks + 1)
                    one = slice(checks, checks + 1)
                    nc.gpsimd.partition_all_reduce(lost_any[:, one], lost_pair[:, one], P,
                                                   bass.bass_isa.ReduceOp.max).then_inc(any_set, 1)
                    checks += 1
                pool.wait_ge(pool_done, n)
                pool.wait_ge(pr_free, PRU[(s, kind, t)] + 1)
                halves = 1 if kind in ("mix", "use_mix") else 2
                for i in range(halves):
                    add = nc.gpsimd.tensor_tensor(out=Xb[:, t, :], in0=Xb[:, t, :],
                                                  in1=yA[:, m % 2, i * D:(i + 1) * D], op=ALU.add)
                    if i < halves - 1:
                        n = done.on(add)
                        pool.wait_ge(pool_done, n)
                add.then_inc(y_set, 1)
                if m + 1 < len(y_parts):
                    pool.wait_ge(y_set, m + 1)
            pool.wait_ge(x1_in, 48)
            for t in range(NT):
                nc.gpsimd.tensor_tensor(out=x1r[:, t * D:(t + 1) * D], in0=x1r[:, t * D:(t + 1) * D],
                                        in1=bet, op=ALU.add).then_inc(xb_set, 1)

        @block.scalar
        def _(act):
            done = Tally(act_done)

            def copy(out_, in_, scale=1.0):
                return nc.scalar.activation(out_, in_, ACT.Copy, scale=scale)

            def normalised(first):
                act.wait_ge(var_set, first + 1)
                nc.scalar.activation(sd[:], ve[:], ACT.Sqrt).then_inc(sqrt_set, 1)
                act.wait_ge(norm_set, first + 1)
                if first:
                    act.wait_ge(pr_full, PR_CS)
                for t in range(NT):
                    nc.scalar.activation(Xn[:, t, :], Xb[:, t, :], ACT.Relu, bias=nmr[:, t:t + 1],
                                         scale=rstd[:, t:t + 1]).then_inc(h_set, 1)

            def flipped(base):
                for q in range(NT // 2):
                    n = base + q
                    act.wait_ge(tr_full, n + 1)
                    copy(XT[:, :, q * 2 * P:(q + 1) * 2 * P],
                         tr[:, n % 2, :].rearrange("p (c n) -> p c n", c=KD)).then_inc(tr_free, 1)

            act.wait_ge(x_in, 16)
            normalised(0)
            flipped(TR_H)
            act.wait_ge(tr_full, TR_W1 + 1)
            copy(W1T[:], tr[0:DA, TR_W1 % 2, 0:D]).then_inc(tr_free, 1)
            act.wait_ge(pr_full, PR_W12 + 1)
            w12 = pr[:, PR_W12 % 2, 0:KD * DA].rearrange("p (c n) -> p c n", c=KD)
            copy(W12[:, :, 0, :], w12)
            copy(W12[:, :, 1, :], w12).then_inc(pr_free, 1)
            for t in range(NT):
                n = PR_H2 + t
                act.wait_ge(pr_full, n + 1)
                copy(h2[:, t, :], pr[:, n % 2, 0:D + 2]).then_inc(pr_free, 1)
            for q in range(NQ):
                n = PR_A2 + q
                act.wait_ge(pr_full, n + 1)
                copy(a2bc[:, q * BANK:(q + 1) * BANK], pr[:, n % 2, :]).then_inc(pr_free, 1)

            def weights(t):
                if t >= 2:
                    act.wait_ge(attq_full, 4 * (t - 1))
                if t == 0:
                    act.wait_ge(pr_free, PR_Y)
                    act.wait_ge(nm_set, 1)
                nc.scalar.activation(att[:, t % 2, :], a2bc[:], ACT.Exp, bias=off1[:, t:t + 1])
                nc.scalar.activation(att2[:, t % 2, :], a2bc[:], ACT.Exp, bias=off2[:, t:t + 1],
                                     scale=ALPHA).then_inc(exp_set, 1)
                act.wait_ge(adj_in[t % 3], 16 * (t // 3 + 1))
                if t >= 2:
                    act.wait_ge(rsum_set, t - 1)
                nc.scalar.activation(junk[:, t % 2, :], adjn[:, t % 3, :], ACT.Copy,
                                     accum_out=rsum[:, t:t + 1]).then_inc(rsum_set, 1)

            def elu_exp(t):
                act.wait_ge(ym_set, t + 1)
                nc.scalar.activation(tA[:, t % 2, :], tA[:, t % 2, :], ACT.Exp).then_inc(ee_set, 1)

            weights(0)
            for t in range(NT):
                if t + 1 < NT:
                    weights(t + 1)
                for q in range(4):
                    n = 4 * t + q
                    act.wait_ge(adjq_full, n + 1)
                    if t >= 2 and q == 0:
                        act.wait_ge(adjT_out[t % 2], 16 * (t // 2))
                    copy(adjT[:, t % 2, q * BANK:(q + 1) * BANK], Lp[:, n % 2, :]).then_inc(adjq_free, 1)
                if t >= 2:
                    elu_exp(t - 2)
            elu_exp(NT - 2)
            elu_exp(NT - 1)
            act.wait_ge(pr_full, PR_CS + 1)
            copy(csum[:], pr[:, PR_CS % 2, 0:NT]).then_inc(pr_free, 1)

            normalised(1)
            flipped(TR_X)
            act.wait_ge(colacc_set, NT)
            for slot in range(2):
                act.wait_ge(adjT_out[slot], 16 * NT // 2)
            for step in range(2):
                moved = 0
                for task in scalar_order(step):
                    kind, t = task[0], task[1]
                    if kind in ("lift_from", "lift", "steer"):
                        two = slice(2 * t, 2 * t + 2)
                        if kind == "lift_from":
                            act.wait_ge(l_free, step * NT + 2 * t + 2)
                            done.on(copy(aim[:, two], Zs[:, two], 2 * P_NUC))
                            moved = done.on(copy(nth[:, two], Zs[:, two], -LOW_END * RATIO[0]))
                            if LIFTS[step] == 0:
                                act.wait_ge(act_done, moved)
                                copy(nth[:, two], nth[:, two]).then_inc(lift_set, 1)
                        if kind == "lift":
                            e = E[:, t % SLOTS, :]
                            act.wait_ge(act_done, max(moved, done.n - 1))
                            done.on(nc.scalar.activation(lifted[:, 0, :], e, ACT.Relu, bias=nth[:, t:t + 1],
                                                         accum_out=above[:, t:t + 1]))
                            act.wait_ge(act_done, max(moved, done.n - 1))
                            done.on(nc.scalar.activation(lifted[:, 1, :], e, ACT.Sign, bias=nth[:, t:t + 1],
                                                         accum_out=signs[:, t:t + 1]))
                        if kind == "steer":
                            k = task[2]
                            up = RATIO[k + 1]
                            down = up / RATIO[k]
                            done.on(copy(nlift0[:, two], nth[:, two], (up + down) / 2))
                            done.on(copy(nlift1[:, two], nth[:, two], (down - up) / 2))
                            for i in (2 * t, 2 * t + 1):
                                one = slice(i, i + 1)
                                n = done.on(nc.scalar.activation(rest[:, one], nth[:, one], ACT.Identity,
                                                                 bias=aim[:, one], scale=float(N)))
                            for i in (2 * t, 2 * t + 1):
                                one = slice(i, i + 1)
                                act.wait_ge(act_done, n)
                                n2 = done.on(nc.scalar.activation(rest[:, one], above[:, one], ACT.Identity,
                                                                  bias=rest[:, one], scale=-2.0))
                            for i in (2 * t, 2 * t + 1):
                                one = slice(i, i + 1)
                                act.wait_ge(act_done, n2 - 1 + i % 2)
                                n3 = done.on(nc.scalar.activation(side_of[:, one], signs[:, one], ACT.Sign,
                                                                  bias=rest[:, one], scale=nth[:, one]))
                            for i in (2 * t, 2 * t + 1):
                                one = slice(i, i + 1)
                                act.wait_ge(act_done, n3 - 1 + i % 2)
                                step_ = nc.scalar.activation(nth[:, one], side_of[:, one], ACT.Identity,
                                                             bias=nlift0[:, one], scale=nlift1[:, one])
                                moved = done.on(step_)
                            if k + 1 == LIFTS[step]:
                                act.wait_ge(act_done, moved)
                                copy(nth[:, two], nth[:, two]).then_inc(lift_set, 1)
                        continue
                    key = (step, kind, t)
                    u, v, m = TRU[key], PRU[key], YU[key]
                    g = step * NT + t
                    if kind in ("gk", "next_gk"):
                        if kind == "next_gk":
                            act.wait_ge(l_full, NT)
                        act.wait_ge(pr_full, v + 1)
                        copy(GT[:, t * BANK:(t + 1) * BANK], pr[:, v % 2, :]).then_inc(pr_free, 1)
                        act.wait_ge(pr_full, v + 2)
                        half, col = t // 2, t % 2
                        part = slice(half * DA, (half + 1) * DA)
                        copy(KT[part, col * BANK:(col + 1) * BANK], pr[part, (v + 1) % 2, :]).then_inc(pr_free, 1)
                    if kind == "logits":
                        act.wait_ge(l_full, g + 1)
                        act.wait_ge(max_set, g + 1)
                        nc.scalar.activation(E[:, t % SLOTS, :], Lp[:].rearrange("p q n -> p (q n)"), ACT.Exp,
                                             bias=nmax[:, t:t + 1],
                                             accum_out=Zs[:, t:t + 1]).then_inc(l_free, 1)
                    if kind == "flip":
                        for q in range(4):
                            act.wait_ge(tr_full, u + q + 1)
                            copy(AT[:, t % 2, q * BANK:(q + 1) * BANK], tr[:, (u + q) % 2, :]).then_inc(tr_free, 1)
                    if kind == "spread" or kind == "mix" and step == 0:
                        k = items.index((kind, t))
                        act.wait_ge(pr_full, v + 1)
                        if kind == "mix":
                            act.wait_ge(rz_set, g // 2 + 1)
                        copy(nat[:, k % 2, :], pr[:, v % 2, 0:D],
                             rz[:, t:t + 1] if kind == "mix" else 1.0).then_inc(pr_free, 1)
                    if kind in ("turn_mix", "turn_spread"):
                        k = items.index((kind[5:], t))
                        act.wait_ge(tr_full, u + 1)
                        where = XT[:, :, t * P:(t + 1) * P] if kind == "turn_mix" else \
                            natT[:, k % 2, :].rearrange("p (c n) -> p c n", c=KD)
                        copy(where, tr[:, u % 2, 0:D].rearrange("p (c n) -> p c n", c=KD)).then_inc(tr_free, 1)
                    if kind in Y_KINDS[step] and m >= 2:
                        act.wait_ge(y_set, m - 1)
                    if kind == "use_mix":
                        act.wait_ge(pr_full, v + 1)
                        copy(yA[:, m % 2, 0:D], pr[:, v % 2, 0:D])
                        copy(V3[:, t, :], pr[:, v % 2, D:2 * D]).then_inc(pr_free, 1)
                    if kind == "mix" and step == 1:
                        act.wait_ge(pr_full, v + 1)
                        act.wait_ge(rz_set, g // 2 + 1)
                        nc.scalar.activation(yA[:, m % 2, 0:D], pr[:, v % 2, 0:D], ACT.Copy,
                                             scale=rz[:, t:t + 1]).then_inc(pr_free, 1)
                    if kind == "use_spread":
                        act.wait_ge(pr_full, v + 1)
                        if t == 0:
                            act.wait_ge(inv_set, 1)
                        for s, where in enumerate((yA[:, m % 2, :], V[:, t, :])):
                            act.wait_ge(pr_full, v + s + 1)
                            b = pr[:, (v + s) % 2, :]
                            copy(where[:, 0:D], b[:, 0:D], rinv[:, t:t + 1])
                            copy(where[:, D:2 * D], b[:, D:2 * D], cinv[:, t:t + 1]).then_inc(pr_free, 1)
                    if kind == "second":
                        act.wait_ge(pr_full, v + 1)
                        b = pr[:, v % 2, :]
                        copy(yA[:, m % 2, 0:D], b[:, 0:D], rinv[:, t:t + 1])
                        copy(yA[:, m % 2, D:2 * D], b[:, D:2 * D],
                             cinv[:, t:t + 1]).then_inc(pr_free, 1)
            act.wait_ge(var_set, 3)
            nc.scalar.activation(sd[:], ve[:], ACT.Sqrt).then_inc(sqrt_set, 1)
            act.wait_ge(norm_set, 3)
            for t in range(NT):
                nc.scalar.activation(Xn[:, t, :], Xb[:, t, :], ACT.Identity, bias=nmr[:, t:t + 1],
                                     scale=rstd[:, t:t + 1]).then_inc(fin_set, 1)

        @block.tensor
        def _(pe):
            pe.wait_ge(consts_set, 2)

            def ring(free, n, depth=2):
                if n >= depth:
                    pe.wait_ge(free, n - depth + 1)

            def flip_rows(base, h_base):
                for q in range(NT // 2):
                    n = base + q
                    pe.wait_ge(h_set, h_base + 2 * q + 2)
                    ring(tr_free, n)
                    for i in range(2):
                        for c in range(KD):
                            last = nc.tensor.transpose(tr[:, n % 2, (2 * c + i) * P:(2 * c + i + 1) * P],
                                                       Xn[:, 2 * q + i, c * P:(c + 1) * P], ident[:])
                    last.then_inc(tr_full, 1)

            flip_rows(TR_H, 0)
            pe.wait_ge(w1_in, 16 * 10)
            ring(tr_free, TR_W1)
            for c in range(KD):
                last = nc.tensor.transpose(tr[0:DA, TR_W1 % 2, c * P:(c + 1) * P], W1s[:, c, :], ident[:])
            last.then_inc(tr_full, 1)
            pe.wait_ge(tr_free, TR_W1 + 1)
            for c in range(KD):
                last = nc.tensor.matmul(pr[:, PR_W12 % 2, c * DA:(c + 1) * DA], W1T[:, c * P:(c + 1) * P], W2s[:],
                                        start=True, stop=True)
            last.then_inc(pr_full, 1)
            pe.wait_ge(wl_set, 2)
            for t in range(NT):
                n = PR_H2 + t
                ring(pr_free, n)
                for c in range(KD):
                    last = nc.tensor.matmul(pr[:, n % 2, 0:D + 2], XT[:, c, t * P:(t + 1) * P], We[:, c, :],
                                            start=c == 0, stop=c == KD - 1)
                last.then_inc(pr_full, 1)
            pe.wait_ge(wl_set, 3)
            for q in range(NQ):
                n = PR_A2 + q
                ring(pr_free, n)
                for c in range(KD):
                    last = nc.tensor.matmul(pr[:, n % 2, :], wrb[:, c, :], XT[:, c, q * BANK:(q + 1) * BANK],
                                            start=c == 0, stop=c == KD - 1)
                last.then_inc(pr_full, 1)

            def flips(t):
                pe.wait_ge(adj_in[t % 3], 16 * (t // 3 + 1))
                for q in range(4):
                    n = 4 * t + q
                    ring(adjq_free, n)
                    for i in range(4):
                        j = (4 * q + i) * P
                        last = nc.tensor.transpose(Lp[:, n % 2, i * P:(i + 1) * P], adjn[:, t % 3, j:j + P], ident[:])
                    last.then_inc(adjq_full, 1)
                pe.wait_ge(att_set, t + 1)
                for q in range(4):
                    n = 4 * t + q
                    ring(attq_free, n)
                    for i in range(4):
                        j = (4 * q + i) * P
                        last = nc.tensor.transpose(Lp[:, 2 + n % 2, i * P:(i + 1) * P], att[:, t % 2, j:j + P], ident[:])
                    last.then_inc(attq_full, 1)

            def product(n, panel, right, width, own=None):
                ring(pr_free, n)
                for j in range(NT):
                    last = nc.tensor.matmul(pr[:, n % 2, 0:width], panel[:, j * P:(j + 1) * P], right[:, j, 0:width],
                                            start=j == 0, stop=j == NT - 1 and own is None)
                if own is not None:
                    last = nc.tensor.matmul(pr[:, n % 2, 0:width], ident[:], own, start=False, stop=True)
                last.then_inc(pr_full, 1)

            flips(0)
            for t in range(NT):
                if t + 1 < NT:
                    flips(t + 1)
                pe.wait_ge(attq_free, 4 * (t + 1))
                product(PR_Y + t, attT[:, t % 2, :], h2, D)
            pe.wait_ge(colacc_set, NT)
            ring(pr_free, PR_CS)
            for j in range(NT):
                last = nc.tensor.matmul(pr[:, PR_CS % 2, j:j + 1], colacc[:, j * P:(j + 1) * P], ones[:, 0:1],
                                        start=True, stop=True)
            last.then_inc(pr_full, 1)

            flip_rows(TR_X, NT)
            np_ = [0]
            for step in range(2):
                for kind, t in ORDER[step]:
                    key = (step, kind, t)
                    u, v = TRU[key], PRU[key]
                    g = step * NT + t
                    if kind in ("gk", "next_gk"):
                        pe.wait_ge(tr_free, TR_X + 2 * (t + 1) if kind == "gk" else TRU[(0, "turn_mix", 4 * t + 3)] + 1)
                        for i, w in enumerate((W12, W3s)):
                            ring(pr_free, v + i)
                            for c in range(KD):
                                last = nc.tensor.matmul(pr[:, (v + i) % 2, :], w[:, c, :, :].rearrange("p a b -> p (a b)"),
                                                        XT[:, c, t * BANK:(t + 1) * BANK],
                                                        start=c == 0, stop=c == KD - 1)
                            last.then_inc(pr_full, 1)
                    if kind == "logits":
                        if g:
                            pe.wait_ge(l_free, g)
                        if t == 0:
                            pe.wait_ge(pr_free, GK_DONE[step])
                        for q in (0, 2, 1, 3):
                            part = slice(q // 2 * DA, (q // 2 + 1) * DA)
                            last = nc.tensor.matmul(Lp[:, q, :], GT[part, t * P:(t + 1) * P],
                                                    KT[part, q % 2 * BANK:(q % 2 + 1) * BANK],
                                                    start=True, stop=True)
                        last.then_inc(l_full, 1)
                    if kind == "flip":
                        pe.wait_ge(keep_set, g + 1)
                        for q in range(4):
                            ring(tr_free, u + q)
                            for i in range(4):
                                j = (4 * q + i) * P
                                last = nc.tensor.transpose(tr[:, (u + q) % 2, i * P:(i + 1) * P],
                                                           E[:, t % SLOTS, j:j + P], ident[:])
                            last.then_inc(tr_full, 1)
                    if kind == "mix":
                        pe.wait_ge(tr_free, TRU[(step, "flip", t)] + 4)
                        product(v, AT[:, t % 2, :], V3 if step else Xn, D)
                    if kind == "spread":
                        pe.wait_ge(st_in[np_[0] % 2], 16 * (np_[0] // 2 + 1))
                        product(v, ST[:, np_[0] % 2, :], Xn, D, own=Xn[:, t, :])
                        np_[0] += 1
                    if kind == "second":
                        pe.wait_ge(pr_free, PRU[(0, "use_spread", NT - 1)] + 2)
                        pe.wait_ge(st_in[np_[0] % 2], 16 * (np_[0] // 2 + 1))
                        product(v, ST[:, np_[0] % 2, :], V, 2 * D, own=V[:, t, :])
                        np_[0] += 1
                    if kind in ("turn_mix", "turn_spread"):
                        product_key = (0, kind[5:], t)
                        k = items.index(product_key[1:])
                        pe.wait_ge(pr_free, PRU[product_key] + 1)
                        ring(tr_free, u)
                        for c in range(KD):
                            last = nc.tensor.transpose(tr[:, u % 2, c * P:(c + 1) * P], nat[:, k % 2, c * P:(c + 1) * P],
                                                       ident[:])
                        last.then_inc(tr_full, 1)
                    if kind in ("use_mix", "use_spread"):
                        turn = "turn_" + kind[4:]
                        k = items.index((kind[4:], t))
                        pe.wait_ge(tr_free, TRU[(0, turn, t)] + 1)
                        for s in range(1 if kind == "use_mix" else 2):
                            ring(pr_free, v + s)
                            for c in range(KD):
                                if kind == "use_mix":
                                    left, right = XT[:, c, t * P:(t + 1) * P], U3s[:, c, :]
                                else:
                                    left, right = natT[:, k % 2, c * P:(c + 1) * P], U12s[:, c, s, :]
                                last = nc.tensor.matmul(pr[:, (v + s) % 2, :], left, right,
                                                        start=c == 0, stop=c == KD - 1)
                            last.then_inc(pr_full, 1)

        @block.vector
        def _(dve):
            done = Tally(vec_done)

            def link(ins):
                done.on(ins)
                dve.wait_ge(vec_done, done.n)

            def stats(t):
                link(nc.vector.bn_stats(st6[:, t, :], Xb[:, t, :]))
                return nc.vector.bn_aggr(mv[:, t, :], st6[:, t, :])

            def scales(n):
                nc.vector.tensor_scalar(out=ve[:], in0=mv[:, :, 1], scalar1=EPS_LN, scalar2=None,
                                        op0=ALU.add).then_inc(var_set, 1)
                dve.wait_ge(sqrt_set, n)
                link(nc.vector.reciprocal(y0[:], sd[:]))
                link(nc.vector.tensor_tensor(out=yt[:], in0=y0[:], in1=y0[:], op=ALU.mult))
                link(nc.vector.tensor_tensor(out=yt[:], in0=yt[:], in1=ve[:], op=ALU.mult))
                link(nc.vector.tensor_scalar(out=yt[:], in0=yt[:], scalar1=-0.5, scalar2=1.5,
                                             op0=ALU.mult, op1=ALU.add))
                link(nc.vector.tensor_tensor(out=rstd[:], in0=y0[:], in1=yt[:], op=ALU.mult))
                nc.vector.scalar_tensor_tensor(out=nmr[:], in0=mv[:, :, 0], scalar=-1.0, in1=rstd[:],
                                               op0=ALU.mult, op1=ALU.mult).then_inc(norm_set, 1)

            dve.wait_ge(x_in, 16)
            for t in range(NT):
                link(stats(t))
            scales(1)
            dve.wait_ge(w0_in, 48)
            for i in range(2):
                for c in range(KD):
                    link(nc.vector.scalar_tensor_tensor(out=wjunk[:], in0=We[:, c, 0:D], scalar=1.0,
                                                        in1=albc[:, i, :], op0=ALU.mult, op1=ALU.mult,
                                                        accum_out=We[:, c, D + i:D + i + 1]))
            nc.vector.memset(wrb[:], 1.0).then_inc(wl_set, 2)
            dve.wait_ge(wl_set, 2)
            for c in range(KD):
                last = nc.vector.tensor_scalar(out=wrb[:, c, :], in0=wrb[:, c, :], scalar1=We[:, c, D + 1:D + 2],
                                               scalar2=None, op0=ALU.mult)
            last.then_inc(wl_set, 1)
            dve.wait_ge(pr_free, PR_Y)
            link(nc.vector.reduce_max(a2max[:], a2bc[:], axis=AX))
            link(nc.vector.tensor_scalar(out=sm[:], in0=h2[:, :, D], scalar1=a2max[:], scalar2=None, op0=ALU.add))
            link(nc.vector.tensor_scalar(out=sm2[:], in0=sm[:], scalar1=ALPHA, scalar2=None, op0=ALU.mult))
            link(nc.vector.tensor_tensor(out=sm[:], in0=sm[:], in1=sm2[:], op=ALU.max))
            done.on(nc.vector.tensor_tensor(out=off1[:], in0=h2[:, :, D], in1=sm[:], op=ALU.subtract))
            nc.vector.scalar_tensor_tensor(out=off2[:], in0=h2[:, :, D], scalar=ALPHA, in1=sm[:], op0=ALU.mult,
                                           op1=ALU.subtract).then_inc(nm_set, 1)

            def elu_parts(t):
                n = PR_Y + t
                dve.wait_ge(pr_full, n + 1)
                if t >= 2:
                    dve.wait_ge(ee_set, t - 1)
                nc.vector.tensor_scalar(out=tA[:, t % 2, :], in0=pr[:, n % 2, 0:D], scalar1=rden[:, t:t + 1],
                                        scalar2=0.0, op0=ALU.mult, op1=ALU.min).then_inc(ym_set, 1)
                nc.vector.tensor_scalar(out=tB[:, t % 2, :], in0=pr[:, n % 2, 0:D], scalar1=rden[:, t:t + 1],
                                        scalar2=0.0, op0=ALU.mult, op1=ALU.max).then_inc(pr_free, 1)

            def residual(t):
                dve.wait_ge(ee_set, t + 1)
                dve.wait_ge(pr_free, PR_Y + t + 1)
                link(nc.vector.scalar_tensor_tensor(out=tB[:, t % 2, :], in0=tA[:, t % 2, :], scalar=-1.0,
                                                    in1=tB[:, t % 2, :], op0=ALU.add, op1=ALU.add))
                nc.vector.tensor_tensor(out=Xb[:, t, :], in0=Xb[:, t, :], in1=tB[:, t % 2, :],
                                        op=ALU.add).then_inc(x1_set, 1)
                dve.wait_ge(x1_set, t + 1)
                link(stats(t))

            for t in range(NT + 3):
                if t < NT:
                    a = att[:, t % 2, :]
                    dve.wait_ge(exp_set, t + 1)
                    dve.wait_ge(adj_in[t % 3], 16 * (t // 3 + 1))
                    link(nc.vector.tensor_tensor(out=a, in0=a, in1=att2[:, t % 2, :], op=ALU.max))
                    nc.vector.scalar_tensor_tensor(out=a, in0=a, scalar=1.0, in1=adjn[:, t % 3, :], op0=ALU.mult,
                                                   op1=ALU.mult, accum_out=deno[:, t:t + 1]).then_inc(att_set, 1)
                    dve.wait_ge(att_set, t + 1)
                    link(nc.vector.tensor_scalar(out=rden[:, t:t + 1], in0=deno[:, t:t + 1], scalar1=EPS_ATT,
                                                 scalar2=None, op0=ALU.add))
                    done.on(nc.vector.reciprocal(rden[:, t:t + 1], rden[:, t:t + 1]))
                    for q in range(4):
                        n = 4 * t + q
                        dve.wait_ge(attq_full, n + 1)
                        if t >= 2 and q == 0:
                            dve.wait_ge(pr_full, PR_Y + t - 1)
                        nc.vector.tensor_copy(attT[:, t % 2, q * BANK:(q + 1) * BANK],
                                              Lp[:, 2 + n % 2, :]).then_inc(attq_free, 1)
                if 2 <= t < NT + 2:
                    elu_parts(t - 2)
                if t >= 3:
                    residual(t - 3)
            scales(2)
            dve.wait_ge(pr_free, PR_CS + 1)
            dve.wait_ge(rsum_set, NT)
            for total, inverse in ((rsum, rinv), (csum, cinv)):
                link(nc.vector.tensor_scalar(out=inverse[:], in0=total[:], scalar1=1.0, scalar2=1e-12,
                                             op0=ALU.add, op1=ALU.max))
                last = nc.vector.reciprocal(inverse[:], inverse[:])
            last.then_inc(inv_set, 1)

            for k in range(STEPS):
                up = RATIO[k + 1] if k + 1 < STEPS else 1.0
                nc.vector.memset(ups[:, k:k + 1], up - up / RATIO[k])
                tables = done.on(nc.vector.memset(downs[:, k:k + 1], up / RATIO[k]))

            def bisect(i, first, widths, rows_of):
                two = slice(2 * i, 2 * i + 2)
                with dve.Fori(first, STEPS, 1) as k:
                    dve.sem_clear(slow_done)
                    for t in (2 * i, 2 * i + 1):
                        nc.vector.scalar_tensor_tensor(out=widths(t), in0=rows_of(t), scalar=th[:, t:t + 1],
                                                       in1=rows_of(t), op0=ALU.is_gt, op1=ALU.mult,
                                                       accum_out=Ms[:, t:t + 1]).then_inc(slow_done, 1)
                    dve.wait_ge(slow_done, 2)
                    nc.vector.tensor_tensor(out=cs[:, two], in0=Ms[:, two], in1=Ts[:, two],
                                            op=ALU.is_ge).then_inc(slow_done, 1)
                    dve.wait_ge(slow_done, 3)
                    nc.vector.tensor_scalar(out=fs[:, two], in0=cs[:, two], scalar1=ups[:, bass.ds(k, 1)],
                                            scalar2=downs[:, bass.ds(k, 1)], op0=ALU.mult,
                                            op1=ALU.add).then_inc(slow_done, 1)
                    dve.wait_ge(slow_done, 4)
                    nc.vector.tensor_tensor(out=th[:, two], in0=th[:, two], in1=fs[:, two],
                                            op=ALU.mult).then_inc(slow_done, 1)
                    dve.wait_ge(slow_done, 5)

            def take(i, flags):
                two = slice(2 * i, 2 * i + 2)
                dve.sem_clear(slow_done)
                nc.vector.tensor_scalar(out=fs[:, two], in0=flags[:, two], scalar1=0.0, scalar2=None,
                                        op0=ALU.is_equal).then_inc(slow_done, 1)
                dve.wait_ge(slow_done, 1)
                nc.vector.tensor_tensor(out=cut[:, two], in0=cut[:, two], in1=fs[:, two],
                                        op=ALU.mult).then_inc(slow_done, 1)
                dve.wait_ge(slow_done, 2)
                nc.vector.tensor_tensor(out=cut[:, two], in0=cut[:, two], in1=th[:, two],
                                        op=ALU.max).then_inc(slow_done, 1)
                dve.wait_ge(slow_done, 3)

            def whole_rows(i):
                two = slice(2 * i, 2 * i + 2)
                dve.sem_clear(slow_done)
                nc.vector.tensor_scalar(out=Ts[:, two], in0=Zs[:, two], scalar1=P_NUC, scalar2=None,
                                        op0=ALU.mult).then_inc(slow_done, 1)
                nc.vector.tensor_scalar(out=th[:, two], in0=Zs[:, two], scalar1=LOW_END * RATIO[0], scalar2=None,
                                        op0=ALU.mult).then_inc(slow_done, 1)
                dve.wait_ge(slow_done, 2)
                bisect(i, 0, lambda t: junk[:, t % 2, :], lambda t: E[:, t % SLOTS, :])
                take(i, lost)

            junk_free, junk2_free = [done.n, done.n], [done.n, done.n]
            dve.wait_ge(vec_done, tables)
            link(nc.vector.memset(st6[:], 0.0))
            for step in range(2):
                coarse = COARSE[step]
                probed, compared, factored, moved = {}, {}, {}, {}
                for unit in search_units(step):
                    kind, i = unit[0], unit[1]
                    two = slice(2 * i, 2 * i + 2)
                    if kind == "max":
                        g = step * NT + i
                        dve.wait_ge(l_full, g + 1)
                        nc.vector.reduce_max(nmax[:, i:i + 1], Lp[:].rearrange("p q n -> p (q n)"), axis=AX,
                                             negate=True).then_inc(max_set, 1)
                    if kind == "begin":
                        dve.wait_ge(l_free, step * NT + 2 * i + 2)
                        done.on(nc.vector.tensor_scalar(out=Ts[:, two], in0=Zs[:, two], scalar1=P_NUC, scalar2=None,
                                                        op0=ALU.mult))
                        start, factor = Zs, LOW_END * RATIO[0]
                        if i > 0:
                            dve.wait_ge(lift_set, step * (NT // 2 - 1) + i)
                            start, factor = nth, -1.0
                        moved[i] = done.on(nc.vector.tensor_scalar(out=th[:, two], in0=start[:, two],
                                                                   scalar1=factor, scalar2=None, op0=ALU.mult))
                    if kind == "probe":
                        e = E[:, i % SLOTS, :]
                        dve.wait_ge(vec_done, max(moved[i // 2], junk_free[i % 2]))
                        probed[i // 2] = junk_free[i % 2] = done.on(nc.vector.scalar_tensor_tensor(
                            out=junk[:, i % 2, :], in0=e, scalar=th[:, i:i + 1], in1=e, op0=ALU.is_gt, op1=ALU.mult,
                            accum_out=Ms[:, i:i + 1]))
                    if kind == "fine":
                        c = cand[:, i % 2, :]
                        dve.wait_ge(vec_done, max(moved[i // 2], junk2_free[i % 2]))
                        probed[i // 2] = junk2_free[i % 2] = done.on(nc.vector.scalar_tensor_tensor(
                            out=junk2[:, i % 2, :], in0=c, scalar=th[:, i:i + 1], in1=c, op0=ALU.is_gt, op1=ALU.mult,
                            accum_out=Ms[:, i:i + 1]))
                    if kind == "compare":
                        dve.wait_ge(vec_done, probed[i])
                        compared[i] = done.on(nc.vector.tensor_tensor(out=cs[:, two], in0=Ms[:, two], in1=Ts[:, two],
                                                                      op=ALU.is_ge))
                    if kind == "factor":
                        k = unit[2]
                        up = RATIO[k + 1] if k + 1 < STEPS else 1.0
                        down = up / RATIO[k]
                        dve.wait_ge(vec_done, compared[i])
                        factored[i] = done.on(nc.vector.tensor_scalar(out=fs[:, two], in0=cs[:, two],
                                                                      scalar1=up - down, scalar2=down,
                                                                      op0=ALU.mult, op1=ALU.add))
                    if kind == "move":
                        dve.wait_ge(vec_done, factored[i])
                        moved[i] = done.on(nc.vector.tensor_tensor(out=th[:, two], in0=th[:, two], in1=fs[:, two],
                                                                   op=ALU.mult))
                    if kind == "collect":
                        if i % 2 == 0:
                            two = slice(i, i + 2)
                            dve.wait_ge(vec_done, moved[i // 2])
                            upper = done.on(nc.vector.tensor_scalar(out=hi[:, two], in0=th[:, two],
                                                                    scalar1=RATIO[coarse] * MARGIN, scalar2=None,
                                                                    op0=ALU.mult))
                            dve.wait_ge(vec_done, upper)
                        for half in range(2):
                            e = E[:, i % SLOTS, half * N // 2:(half + 1) * N // 2]
                            dve.wait_ge(vec_done, max(junk_free))
                            masked = done.on(nc.vector.scalar_tensor_tensor(
                                out=mbuf[:], in0=e, scalar=hi[:, i:i + 1], in1=e, op0=ALU.is_le, op1=ALU.mult,
                                accum_out=tails[:, half, i:i + 1]))
                            dve.wait_ge(vec_done, masked)
                            for j in range(NSEG // 2):
                                at_ = (half * NSEG // 2 + j) * 8
                                collected = done.on(nc.vector.max(out=cand[:, i % 2, at_:at_ + 8],
                                                                  in_=mbuf[:, j * SEG:(j + 1) * SEG]))
                            junk_free = [collected, collected]
                    if kind == "resolve":
                        pair = step * NT // 2 + i
                        dve.wait_ge(vec_done, collected)
                        link(nc.vector.tensor_tensor(out=Ts[:, two], in0=tails[:, 0, two], in1=tails[:, 1, two],
                                                     op=ALU.add))
                        done.on(nc.vector.scalar_tensor_tensor(out=Ts[:, two], in0=Zs[:, two], scalar=P_NUC - 1,
                                                               in1=Ts[:, two], op0=ALU.mult, op1=ALU.add))
                        link(nc.vector.reduce_max(
                            eighth[:, two], cand[:].rearrange("p s (g e) -> p s g e", e=8)[:, :, :, 7],
                            axis=AX))
                        done.on(nc.vector.scalar_tensor_tensor(out=lost[:, two], in0=eighth[:, two],
                                                               scalar=RATIO[coarse] * MARGIN, in1=th[:, two],
                                                               op0=ALU.mult, op1=ALU.is_ge))
                    if kind == "finish":
                        pair = step * NT // 2 + i
                        dve.wait_ge(vec_done, moved[i])
                        link(nc.vector.tensor_scalar(out=hi[:, two], in0=th[:, two],
                                                     scalar1=RATIO[FINE[step]] * MARGIN, scalar2=None, op0=ALU.mult))
                        for t in (2 * i, 2 * i + 1):
                            c = cand[:, t % 2, :]
                            dve.wait_ge(vec_done, junk2_free[t % 2])
                            junk2_free[t % 2] = done.on(nc.vector.scalar_tensor_tensor(
                                out=junk2[:, t % 2, :], in0=c, scalar=hi[:, t:t + 1], in1=c, op0=ALU.is_gt,
                                op1=ALU.mult, accum_out=Ms[:, t:t + 1]))
                        for t in (2 * i, 2 * i + 1):
                            c = cand[:, t % 2, :]
                            dve.wait_ge(vec_done, junk2_free[t % 2])
                            masked = done.on(nc.vector.scalar_tensor_tensor(out=c, in0=c, scalar=hi[:, t:t + 1], in1=c,
                                                                            op0=ALU.is_le, op1=ALU.mult))
                        for t in (2 * i, 2 * i + 1):
                            dve.wait_ge(vec_done, masked - 1 + t % 2)
                            tops = done.on(nc.vector.max(out=top8[:, t % 2, 8:16], in_=cand[:, t % 2, :]))
                        done.on(nc.vector.tensor_tensor(out=Ts[:, two], in0=Ts[:, two], in1=Ms[:, two],
                                                        op=ALU.subtract))
                        dve.wait_ge(vec_done, tops)
                        n = done.on(nc.vector.tensor_tensor(out=sum2[:, :, 8:16], in0=top8[:, :, 8:16],
                                                            in1=top8[:, :, 7:15], op=ALU.add))
                        dve.wait_ge(vec_done, n - 1)
                        done.on(nc.vector.tensor_scalar(out=Ts[:, two], in0=Ts[:, two], scalar1=1e-30, scalar2=None,
                                                        op0=ALU.max))
                        dve.wait_ge(vec_done, n)
                        link(nc.vector.tensor_tensor(out=sum4[:, :, 8:16], in0=sum2[:, :, 8:16],
                                                     in1=sum2[:, :, 6:14], op=ALU.add))
                        link(nc.vector.tensor_tensor(out=sum2[:, :, 8:16], in0=sum4[:, :, 8:16],
                                                     in1=sum4[:, :, 4:12], op=ALU.add))
                        n2 = done.on(nc.vector.tensor_tensor(
                            out=sum4[:, :, 8:16], in0=sum2[:, :, 7:15],
                            in1=Ts[:, two].rearrange("p (s o) -> p s o", o=1).to_broadcast([P, 2, 8]), op=ALU.is_ge))
                        dve.wait_ge(vec_done, n2)
                        n2 = done.on(nc.vector.scalar_tensor_tensor(out=sum4[:, :, 8:16], in0=sum4[:, :, 8:16],
                                                                    scalar=-4.0, in1=top8[:, :, 8:16], op0=ALU.mult,
                                                                    op1=ALU.subtract))
                        dve.wait_ge(vec_done, n2)
                        cut_set = done.on(nc.vector.reduce_max(cut[:, two], sum4[:, :, 8:16], axis=AX, negate=True))
                        dve.wait_ge(vec_done, cut_set)
                        for t in (2 * i, 2 * i + 1):
                            c = cand[:, t % 2, :]
                            junk2_free[t % 2] = done.on(nc.vector.scalar_tensor_tensor(
                                out=junk2[:, t % 2, :], in0=c, scalar=cut[:, t:t + 1], in1=c, op0=ALU.is_ge,
                                op1=ALU.mult, accum_out=Ms[:, t:t + 1]))
                        dve.wait_ge(vec_done, max(junk2_free))
                        link(nc.vector.scalar_tensor_tensor(out=eighth[:, two], in0=Ms[:, two], scalar=MARGIN,
                                                            in1=Ts[:, two], op0=ALU.mult, op1=ALU.is_lt))
                        link(nc.vector.scalar_tensor_tensor(out=lost[:, two], in0=lost[:, two], scalar=2.0,
                                                            in1=eighth[:, two], op0=ALU.mult, op1=ALU.max))
                        nc.vector.reduce_max(lost_pair[:, pair:pair + 1], lost[:, two], axis=AX).then_inc(lost_set, 1)
                    if kind == "check":
                        pair = step * NT // 2 + i
                        dve.wait_ge(any_set, pair + 1)
                        any_lost = dve.value_load(lost_any[0:1, pair:pair + 1], min_val=0, max_val=2)
                        with dve.If(any_lost > 0):
                            dve.wait_ge(vec_done, max(cut_set, *junk2_free))
                            bisect(i, FINE[step], lambda t: junk2[:, t % 2, :], lambda t: cand[:, t % 2, :])
                            take(i, eighth)
                            with dve.If(any_lost > 1):
                                dve.wait_ge(vec_done, max(junk_free))
                                whole_rows(i)
                    if kind == "keep":
                        dve.wait_ge(vec_done, cut_set)
                        for t in (2 * i, 2 * i + 1):
                            e = E[:, t % SLOTS, :]
                            nc.vector.scalar_tensor_tensor(out=e, in0=e, scalar=cut[:, t:t + 1], in1=e, op0=ALU.is_ge,
                                                           op1=ALU.mult, accum_out=Zk[:, t:t + 1]).then_inc(keep_set, 1)
                        dve.wait_ge(keep_set, step * NT + 2 * i + 2)
                        nc.vector.reciprocal(rz[:, two], Zk[:, two]).then_inc(rz_set, 1)
            for t in range(NT):
                dve.wait_ge(y_set, YU[(1, "mix", t)] + 1)
                link(stats(t))
            scales(3)
            dve.wait_ge(x1_in, 48)
            for t in range(NT):
                dve.wait_ge(fin_set, t + 1)
                link(nc.vector.tensor_tensor(out=Xn[:, t, :], in0=Xn[:, t, :], in1=gam, op=ALU.mult))
                dve.wait_ge(xb_set, t + 1)
                nc.vector.tensor_tensor(out=Xb[:, t, :], in0=Xn[:, t, :], in1=x1r[:, t * D:(t + 1) * D],
                                        op=ALU.add).then_inc(out_set, 1)


_INS = ["x", "adj", "L0_gnn_W", "L0_gnn_attn_l", "L0_gnn_attn_r", "L1_gnn_W1", "L1_gnn_W2", "L1_gnn_W3",
        "L1_gnn_U1", "L1_gnn_U2", "L1_gnn_U3", "L1_gnn_gamma", "L1_gnn_beta"]


def kernel(**inputs):
    import numpy as np
    import concourse.bacc as bacc
    from concourse.bass_utils import run_bass_kernel_spmd

    nc = bacc.Bacc("TRN2", target_bir_lowering=False, num_devices=1)
    arrays, args = {}, []
    for name in _INS:
        a = np.ascontiguousarray(inputs[name])
        arrays[f"in_{name}"] = a
        args.append(nc.dram_tensor(f"in_{name}", a.shape, mybir.dt.from_np(a.dtype), kind="ExternalInput").ap())
    out = nc.dram_tensor("out", (N, D), mybir.dt.float32, kind="ExternalOutput").ap()
    build(nc, *args, out)
    r = run_bass_kernel_spmd(nc, [arrays], core_ids=[0])
    return r.results[0]["out"]
```

```python
import concourse.bass as bass
import concourse.mybir as mybir
from concourse.alu_op_type import AluOpType as ALU

N = 2048
D = 256
DA = 64
P = 128
NT = N // P
KD = D // P
BANK = 512
NQ = N // BANK
ALPHA = 0.2
EPS_ATT = 1e-9
EPS_LN = 1e-5
P_NUC = 0.9

LOG2_RANGE = 15.0
STEPS = 20
RATIO = [2.0 ** (LOG2_RANGE / 2 ** (k + 1)) for k in range(STEPS)]
LOW_END = (1 - P_NUC) / N * (1 - 1e-5)
COARSE = (5, 8)
FINE = (8, 12)
LIFTS = (2, 4)
MARGIN = 1 + 1e-6
SLOTS = 4
SEG = 64
NSEG = N // SEG
NC = 8 * NSEG

SIDE_FIRST = (4, 4)
FIRST_BETWEEN = ((1, 1, 3, 0), (0, 0, 0, 4))
EARLY = (2, 1)
LIFTS_BEFORE = ({"mix": 1, "spread": 1, "use_mix": 1, "use_spread": 1}, {"mix": 1, "second": 3})
PLACES = ((3, 3, 16), (0, 0, 8))
CHECK_EARLY = 2
H2_FIRST = 6
OUT_PARTS = ((0, NT // 2 - 1), (NT // 2 - 1, NT - 2), (NT - 2, NT))


def staggered(items):
    tasks = []
    for i in range(len(items) + 2):
        for lag, what in enumerate(("", "turn_", "use_")):
            if 0 <= i - lag < len(items):
                kind, t = items[i - lag]
                tasks.append((what + kind, t))
    return tasks


def order_of_step(step):
    side = [("spread" if step == 0 else "second", t) for t in range(NT)]
    first, side = side[:SIDE_FIRST[step]], side[SIDE_FIRST[step]:]
    first = staggered(first) if step == 0 else first
    tasks = []
    if step == 0:
        tasks += [("xt", q) for q in range(6)] + [("gk", 0), ("gk", 1), ("xt", 6), ("xt", 7), ("gk", 2), ("gk", 3)]
    for t, n in zip(range(SLOTS), FIRST_BETWEEN[step]):
        tasks += [("logits", t)] + first[:n]
        first = first[n:]
    tasks += first
    for a in range(0, NT, 2):
        logits = [("logits", t + SLOTS) for t in (a, a + 1) if t + SLOTS < NT]
        mixes = [("mix", a), ("mix", a + 1)]
        now, side = side[:2], side[2:]
        for logit in logits[:1]:
            tasks.insert(len(tasks) - EARLY[step], logit)
        tasks += [("flip", a), ("flip", a + 1)] + logits[1:]
        if step == 0:
            if a == NT - 2:
                tasks += mixes + [("turn_" + k, t) for k, t in mixes] + [("next_gk", NQ - 1)]
                tasks += [("use_" + k, t) for k, t in mixes]
            else:
                tasks += staggered(mixes + now)
            if a == NT - 4:
                tasks += [("next_gk", q) for q in range(NQ - 1)]
        else:
            tasks += mixes[:1] + now[:1] + mixes[1:] + now[1:]
    assert not side
    return tasks


ORDER = [order_of_step(0), order_of_step(1)]


def scalar_order(step):
    tasks, lifts = [], []
    order = list(ORDER[step])
    for t in range(0, NT - SLOTS, 2):
        order.remove(("logits", t + SLOTS))
        order.insert(order.index(("flip", t)) + 1, ("logits", t + SLOTS))
    for kind, t in order:
        if kind in LIFTS_BEFORE[step]:
            for _ in range(LIFTS_BEFORE[step][kind]):
                if lifts:
                    tasks.append(lifts.pop(0))
                    if lifts and lifts[0][0] == "steer":
                        tasks.append(lifts.pop(0))
        if kind == "flip" and t % 2 == 0:
            tasks += lifts
            lifts = []
        tasks.append((kind, t))
        if kind == "logits" and t % 2 and t > 1:
            q = t // 2
            tasks.append(("lift_from", q))
            for k in range(LIFTS[step]):
                lifts += [("lift", t - 1, k), ("lift", t, k), ("steer", q, k)]
    return tasks


def coarse_units(q, coarse, first):
    units = [("begin", q)]
    for k in range(first, coarse):
        units += [("probe", 2 * q, k), ("probe", 2 * q + 1, k)]
        units += [("compare", q, k), ("factor", q, k), ("move", q, k)]
    return units


def search_units(step):
    coarse, lifts = COARSE[step], LIFTS[step]
    pairs = NT // 2
    units = [("max", 0), ("max", 1)]
    ahead = coarse_units(0, coarse, 0)
    units += ahead[:6] + [("max", 2)] + ahead[6:11] + [("max", 3)] + ahead[11:]
    for q in range(pairs):
        units += [("collect", 2 * q), ("collect", 2 * q + 1), ("resolve", q)]
        for k in range(coarse, FINE[step]):
            units += [("fine", 2 * q, k), ("fine", 2 * q + 1, k), ("compare", q, k), ("factor", q, k), ("move", q, k)]
        units += [("finish", q)]
        ahead = coarse_units(q + 1, coarse, lifts) if q + 1 < pairs else []
        more = q + 2 < pairs
        before, check, after = PLACES[step]
        units += ahead[:before] + [("max", 2 * q + 4)] * more + ahead[before:check]
        units += [("check", q), ("keep", q)] + ahead[check:after] + [("max", 2 * q + 5)] * more + ahead[after:]
    return units


class Tally:

    def __init__(self, sem):
        self.sem, self.n = sem, 0

    def on(self, ins, by=1):
        self.n += by
        ins.then_inc(self.sem, by)
        return self.n


def build(nc, x, adj, W, attn_l, attn_r, W1, W2, W3, U1, U2, U3, gamma, beta, out):
    from contextlib import ExitStack
    f32 = mybir.dt.float32
    ACT = mybir.ActivationFunctionType
    AX = mybir.AxisListType.X

    adjT_dram = nc.dram_tensor("adjT_scratch", [NT, P, NT * P], f32, kind="Internal").ap()
    x1_dram = nc.dram_tensor("x1_scratch", [P, NT * D], f32, kind="Internal").ap()
    rows = lambda ap: ap.rearrange("(t p) d -> p t d", p=P)

    with ExitStack() as ctx:
        def sb(name, shape):
            return ctx.enter_context(nc.sbuf_tensor(name, shape, f32))

        def sem(name):
            return ctx.enter_context(nc.semaphore(name))

        ident = sb("ident", [P, P])
        ones = sb("ones", [P, 2])
        Xn = sb("Xn", [P, NT, D])
        XT = sb("XT", [P, KD, N])
        Xb = sb("Xb", [P, NT, D])
        W12 = sb("W12", [P, KD, 2, DA])
        W3s = sb("W3s", [P, KD, 2, DA])
        U12s = sb("U12s", [P, KD, 2, 2 * D])
        U3s = sb("U3s", [P, KD, 2 * D])
        st6 = sb("st6", [P, NT, 6])
        mv = sb("mv", [P, NT, 2])
        ve = sb("ve", [P, NT])
        sd = sb("sd", [P, NT])
        y0 = sb("y0", [P, NT])
        yt = sb("yt", [P, NT])
        rstd = sb("rstd", [P, NT])
        nmr = sb("nmr", [P, NT])
        a2max = sb("a2max", [P, 1])
        sm = sb("sm", [P, NT])
        sm2 = sb("sm2", [P, NT])
        off1 = sb("off1", [P, NT])
        off2 = sb("off2", [P, NT])
        deno = sb("deno", [P, NT])
        rden = sb("rden", [P, NT])
        rsum = sb("rsum", [P, NT])
        rinv = sb("rinv", [P, NT])
        csum = sb("csum", [P, NT])
        cinv = sb("cinv", [P, NT])
        nmax = sb("nmax", [P, NT])
        Zs = sb("Zs", [P, NT])
        Ts = sb("Ts", [P, NT])
        th = sb("th", [P, NT])
        Ms = sb("Ms", [P, NT])
        cs = sb("cs", [P, NT])
        fs = sb("fs", [P, NT])
        Zk = sb("Zk", [P, NT])
        rz = sb("rz", [P, NT])
        ups = sb("ups", [P, STEPS])
        downs = sb("downs", [P, STEPS])
        mbuf = sb("mbuf", [P, N // 2])
        cand = sb("cand", [P, 2, NC])
        tails = sb("tails", [P, 2, NT])
        hi = sb("hi", [P, NT])
        eighth = sb("eighth", [P, NT])
        lost = sb("lost", [P, NT])
        lost_pair = sb("lost_pair", [P, NT])
        lost_any = ctx.enter_context(nc.sbuf_tensor("lost_any", [P, NT], mybir.dt.int32))
        arena = sb("arena", [P, 33792])
        at = [0]

        def view(words):
            v = arena[:, at[0]:at[0] + words]
            at[0] += words
            return v

        h2 = view(NT * (D + 1)).rearrange("p (t d) -> p t d", t=NT)
        a2bc = view(N)
        adjn = view(3 * N).rearrange("p (s n) -> p s n", s=3)
        att = view(2 * N).rearrange("p (s n) -> p s n", s=2)
        att2 = view(2 * N).rearrange("p (s n) -> p s n", s=2)
        adjT = view(2 * N).rearrange("p (s n) -> p s n", s=2)
        attT = view(2 * N).rearrange("p (s n) -> p s n", s=2)
        colacc = view(N)
        wrb = view(KD * P).rearrange("p (c n) -> p c n", c=KD)
        albc = view(2 * D).rearrange("p (s n) -> p s n", s=2)
        wjunk = view(D)
        We = view(KD * (D + 2)).rearrange("p (c n) -> p c n", c=KD)
        tA = view(2 * D).rearrange("p (s n) -> p s n", s=2)
        tB = view(2 * D).rearrange("p (s n) -> p s n", s=2)
        W1s = view(KD * DA).rearrange("p (c n) -> p c n", c=KD)
        W1T = view(D)[0:DA, :]
        W2s = view(DA)[0:DA, :]
        lifted = ctx.enter_context(nc.sbuf_tensor("lifted", [P, 4 * D], f32))
        wlb = lifted[:, 0:D].rearrange("p (c n) -> p c n", c=KD)
        wlbc = lifted[:, D:2 * D]
        a1junk = lifted[:, 2 * D:4 * D].rearrange("p (s n) -> p s n", s=2)
        lifted = lifted[:].bitcast(mybir.dt.uint8).rearrange("p (s n) -> p s n", s=2)
        at[0] = 0
        V = view(NT * 2 * D).rearrange("p (t d) -> p t d", t=NT)
        V3 = view(NT * D).rearrange("p (t d) -> p t d", t=NT)
        GT = view(N)
        KT = view(N // 2)
        E = view(SLOTS * N).rearrange("p (s n) -> p s n", s=SLOTS)
        AT = view(2 * N).rearrange("p (s n) -> p s n", s=2)
        ST = view(2 * N).rearrange("p (s n) -> p s n", s=2)
        nat = view(2 * D).rearrange("p (s n) -> p s n", s=2)
        natT = view(2 * D).rearrange("p (s n) -> p s n", s=2)
        yA = view(2 * 2 * D).rearrange("p (s n) -> p s n", s=2)
        x1r = arena[:, 0:NT * D]
        top8, sum2, sum4 = (st6[:].rearrange("p a b -> p (a b)")[:, 32 * i:32 * i + 32].rearrange("p (s n) -> p s n", s=2)
                            for i in range(3))
        cut = yt
        gam = arena[:, NT * D:NT * D + D]
        bet = arena[:, NT * D + D:NT * D + 2 * D]
        nth, aim, above, signs, rest, nlift0, nlift1, side_of = off1, off2, deno, rden, sm, sm2, rsum, csum

        junk = mbuf[:].bitcast(mybir.dt.uint8).rearrange("p (s n) -> p s n", s=2)
        junk2 = ctx.enter_context(nc.sbuf_tensor("junk2", [P, 2, NC], mybir.dt.uint8))
        Lp = ctx.enter_context(nc.psum_tensor("Lp", [P, NQ, BANK], f32))
        pr = ctx.enter_context(nc.psum_tensor("pr", [P, 2, BANK], f32))
        tr = ctx.enter_context(nc.psum_tensor("tr", [P, 2, BANK], f32))

        w0_in, w1_in, x1_out, x1_in = map(sem, "w0_in w1_in x1_out x1_in".split())
        x_in = [sem(f"x_in{i}") for i in range(4)]
        y_out = sem("y_out")
        adj_in = [sem(f"adj_in{i}") for i in range(3)]
        adjT_out = [sem(f"adjT_out{i}") for i in range(2)]
        st_in = [sem(f"st_in{i}") for i in range(2)]
        consts_set = sem("consts_set")
        var_set = sem("var_set")
        sqrt_set = sem("sqrt_set")
        norm_set = sem("norm_set")
        h_set = sem("h_set")
        wl_set = sem("wl_set")
        nm_set = sem("nm_set")
        exp_set = sem("exp_set")
        att_set = sem("att_set")
        rsum_set = sem("rsum_set")
        colacc_set = sem("colacc_set")
        adjq_full, adjq_free = sem("adjq_full"), sem("adjq_free")
        attq_full, attq_free = sem("attq_full"), sem("attq_free")
        tr_full, tr_free = sem("tr_full"), sem("tr_free")
        pr_full, pr_free = sem("pr_full"), sem("pr_free")
        l_full, l_free = sem("l_full"), sem("l_free")
        max_set = sem("max_set")
        keep_set = sem("keep_set")
        lift_set = sem("lift_set")
        lost_set, any_set = sem("lost_set"), sem("any_set")
        slow_done = sem("slow_done")
        rz_set = sem("rz_set")
        ym_set, ee_set, x1_set = sem("ym_set"), sem("ee_set"), sem("x1_set")
        y_set = sem("y_set")
        eye_set = sem("eye_set")
        inv_set = sem("inv_set")
        xb_set = sem("xb_set")
        out_set = sem("out_set")
        vec_done, act_done, pool_done = sem("vec_done"), sem("act_done"), sem("pool_done")

        TR_H = 0
        TR_W1 = TR_H + NT // 2
        TR_X = TR_W1 + 1
        PR_WL = 0
        PR_A2 = PR_WL + 1
        PR_W12 = PR_A2 + NQ
        PR_H2 = PR_W12 + 1
        PR_Y = PR_H2 + NT
        PR_CS = PR_Y + NT
        PR_GK = PR_CS + 1
        Y_KINDS = (("use_mix", "use_spread"), ("mix", "second"))
        uses = {"xt": (1, 0, 0), "gk": (0, 2, 0), "next_gk": (0, 2, 0), "logits": (0, 0, 0), "flip": (4, 0, 0),
                "mix": (0, 1, 0), "turn_mix": (1, 0, 0), "use_mix": (0, 1, 1),
                "spread": (0, 1, 0), "turn_spread": (1, 0, 0), "use_spread": (0, 2, 1), "second": (0, 1, 1)}
        TRU, PRU, YU = {}, {}, {}
        ntr, npr, ny = TR_X, PR_GK, 0
        for step in range(2):
            for kind, t in ORDER[step]:
                key = (step, kind, t)
                TRU[key], PRU[key], YU[key] = ntr, npr, ny
                a, b, c = uses[kind] if (step == 0 or kind != "mix") else (0, 1, 1)
                ntr, npr, ny = ntr + a, npr + b, ny + c
        GK_DONE = [PRU[(0, "gk", NQ - 1)] + 2, PRU[(0, "next_gk", NQ - 1)] + 2]
        LN_PARTS = ((0, NT), (0, NT - 4), (NT - 4, NT), (0, NT - 2), (NT - 2, NT))
        items = [(k, t) for k, t in ORDER[0] if k in ("mix", "spread")]
        y_parts = [(s, k, t) for s in range(2) for k, t in ORDER[s] if k in Y_KINDS[s]]
        panels = [(s, k, t) for s in range(2) for k, t in ORDER[s] if k in ("spread", "second")]

        CHECK_BEFORE, seen, sides = [], 0, 0
        for s in range(2):
            for kind, t in ORDER[s]:
                if kind == "flip" and t % 2 == 0:
                    seen = s * NT // 2 + t // 2 + 1
                    for m in range(len(CHECK_BEFORE) - min(CHECK_EARLY, sides), len(CHECK_BEFORE)):
                        CHECK_BEFORE[m] = seen
                    sides = 0
                if kind in Y_KINDS[s]:
                    CHECK_BEFORE.append(seen)
                    sides += kind in ("use_spread", "second")

        block = ctx.enter_context(nc.Block())

        @block.sync
        def _(sp):
            sp.dma_start(We[:, :, 0:D], rows(W)).then_inc(w0_in, 16)
            for i, a in enumerate((attn_l, attn_r)):
                sp.dma_start(albc[:, i, :],
                             a.rearrange("d o -> o d").to_broadcast([P, D])).then_inc(w0_in, 16)

            for i in range(4):
                part = slice(i * NT // 4, (i + 1) * NT // 4)
                sp.dma_start(Xb[:, part, :], rows(x)[:, part, :]).then_inc(x_in[i], 16)

            def load_adj(t):
                if t >= 3:
                    u = t - 2
                    sp.wait_ge(att_set, u)
                    sp.wait_ge(rsum_set, u)
                    sp.wait_ge(colacc_set, u)
                    sp.wait_ge(adjq_full, 4 * u)
                sp.dma_start(adjn[:, t % 3, :], adj[t * P:(t + 1) * P, :]).then_inc(adj_in[t % 3], 16)

            load_adj(0)
            sp.dma_start(W1s[:], rows(W1)).then_inc(w1_in, 16)
            sp.dma_start(W2s[:], W2).then_inc(w1_in, 16)
            for i in range(2):
                sp.dma_start(W3s[:, :, i, :], rows(W3)).then_inc(w1_in, 16)
            for s in range(2):
                sp.dma_start(U12s[:, :, s, 0:D], rows(U1[s])).then_inc(w1_in, 16)
                sp.dma_start(U12s[:, :, s, D:2 * D], rows(U2[s])).then_inc(w1_in, 16)
                sp.dma_start(U3s[:, :, s * D:(s + 1) * D], rows(U3[s])).then_inc(w1_in, 16)
            load_adj(1)
            load_adj(2)
            for t in range(NT):
                sp.wait_ge(eye_set, t + 1)
                sp.dma_start(adjT_dram[t], adjT[:, t % 2, :]).then_inc(adjT_out[t % 2], 16)
                if t + 3 < NT:
                    load_adj(t + 3)
            sp.wait_ge(x1_set, NT)
            sp.dma_start(x1_dram, Xb[:].rearrange("p t d -> p (t d)")).then_inc(x1_out, 16)
            for s in range(2):
                sp.wait_ge(adjT_out[s], 16 * NT // 2)
            sp.wait_ge(h_set, 2 * NT)
            sp.wait_ge(pr_free, PR_CS + 1)
            for n, panel in enumerate(panels):
                if n >= 2:
                    sp.wait_ge(pr_full, PRU[panels[n - 2]] + 1)
                sp.dma_start(ST[:, n % 2, :], adjT_dram[panel[2]]).then_inc(st_in[n % 2], 16)
            sp.wait_ge(pr_full, PRU[panels[-1]] + 1)
            sp.wait_ge(x1_out, 16)
            sp.dma_start(gam, gamma.rearrange("(o d) -> o d", o=1).to_broadcast([P, D])).then_inc(x1_in, 16)
            sp.dma_start(bet, beta.rearrange("(o d) -> o d", o=1).to_broadcast([P, D])).then_inc(x1_in, 16)
            sp.dma_start(x1r, x1_dram).then_inc(x1_in, 16)
            for first, end in OUT_PARTS:
                sp.wait_ge(out_set, end)
                sp.dma_start(rows(out)[:, first:end, :], Xb[:, first:end, :]).then_inc(y_out, 16)
            sp.wait_ge(y_out, 16 * len(OUT_PARTS))

        @block.gpsimd
        def _(pool):
            done = Tally(pool_done)
            n = done.on(nc.gpsimd.memset(ident[:], 0.0))
            nc.gpsimd.memset(ones[:], 1.0).then_inc(consts_set, 1)
            pool.wait_ge(pool_done, n)
            nc.gpsimd.affine_select(out=ident[:], in_=ident[:], compare_op=ALU.not_equal, fill=1.0, base=0,
                                    pattern=[[-1, P]], channel_multiplier=1).then_inc(consts_set, 1)
            for t in range(NT):
                pool.wait_ge(adj_in[t % 3], 16 * (t // 3 + 1))
                if t == 0:
                    nc.gpsimd.tensor_copy(colacc[:], adjn[:, 0, :]).then_inc(colacc_set, 1)
                else:
                    pool.wait_ge(colacc_set, t)
                    nc.gpsimd.tensor_tensor(out=colacc[:], in0=colacc[:], in1=adjn[:, t % 3, :],
                                            op=ALU.add).then_inc(colacc_set, 1)
                pool.wait_ge(adjq_free, 4 * (t + 1))
                own = adjT[:, t % 2, t * P:(t + 1) * P]
                nc.gpsimd.tensor_tensor(out=own, in0=own, in1=ident[:], op=ALU.add).then_inc(eye_set, 1)
            pool.wait_ge(x1_out, 16)
            pool.wait_ge(h_set, 2 * NT)
            n = done.on(nc.gpsimd.tensor_copy(Xb[:], Xn[:]))
            checks = 0
            for m, (s, kind, t) in enumerate(y_parts):
                while checks < CHECK_BEFORE[m]:
                    pool.wait_ge(lost_set, checks + 1)
                    one = slice(checks, checks + 1)
                    nc.gpsimd.partition_all_reduce(lost_any[:, one], lost_pair[:, one], P,
                                                   bass.bass_isa.ReduceOp.max).then_inc(any_set, 1)
                    checks += 1
                    if checks == NT:
                        pool.wait_ge(x1_in, 48)
                        for i in range(NT):
                            part = x1r[:, i * D:(i + 1) * D]
                            nc.gpsimd.tensor_tensor(out=part, in0=part, in1=bet, op=ALU.add).then_inc(xb_set, 1)
                pool.wait_ge(pool_done, n)
                pool.wait_ge(pr_free, PRU[(s, kind, t)] + 1)
                halves = 1 if kind in ("mix", "use_mix") else 2
                for i in range(halves):
                    add = nc.gpsimd.tensor_tensor(out=Xb[:, t, :], in0=Xb[:, t, :],
                                                  in1=yA[:, m % 2, i * D:(i + 1) * D], op=ALU.add)
                    if i < halves - 1:
                        n = done.on(add)
                        pool.wait_ge(pool_done, n)
                add.then_inc(y_set, 1)
                if m + 1 < len(y_parts):
                    pool.wait_ge(y_set, m + 1)

        @block.scalar
        def _(act):
            done = Tally(act_done)

            def copy(out_, in_, scale=1.0):
                return nc.scalar.activation(out_, in_, ACT.Copy, scale=scale)

            def roots(n):
                a, b = LN_PARTS[n]
                act.wait_ge(var_set, n + 1)
                nc.scalar.activation(sd[:, a:b], ve[:, a:b], ACT.Sqrt).then_inc(sqrt_set, 1)

            def normalise(t):
                nc.scalar.activation(Xn[:, t, :], Xb[:, t, :], ACT.Relu, bias=nmr[:, t:t + 1],
                                     scale=rstd[:, t:t + 1]).then_inc(h_set, 1)

            def flipped(n, q):
                act.wait_ge(tr_full, n + 1)
                copy(XT[:, :, q * 2 * P:(q + 1) * 2 * P],
                     tr[:, n % 2, :].rearrange("p (c n) -> p c n", c=KD)).then_inc(tr_free, 1)

            def a2_row(q):
                n = PR_A2 + q
                act.wait_ge(pr_full, n + 1)
                copy(a2bc[:, q * BANK:(q + 1) * BANK], pr[:, n % 2, :]).then_inc(pr_free, 1)

            def h2_rows(t):
                n = PR_H2 + t
                act.wait_ge(pr_full, n + 1)
                copy(h2[:, t, 0:D], pr[:, n % 2, 0:D]).then_inc(pr_free, 1)

            act.wait_ge(consts_set, 2)
            nc.scalar.activation(nmr[:, 0:2], ones[:], ACT.Sqrt)
            act.wait_ge(pr_full, PR_WL + 1)
            copy(wlbc, pr[:, PR_WL % 2, 0:D]).then_inc(pr_free, 1)
            roots(0)
            act.wait_ge(norm_set, 1)
            for c in range(4):
                for t in range(4 * c, 4 * c + 4):
                    normalise(t)
                for q in (2 * c, 2 * c + 1):
                    flipped(TR_H + q, q)
                if c:
                    a2_row(c - 1)
            a2_row(3)
            act.wait_ge(tr_full, TR_W1 + 1)
            copy(W1T, tr[0:DA, TR_W1 % 2, 0:D]).then_inc(tr_free, 1)
            act.wait_ge(pr_full, PR_W12 + 1)
            w12 = pr[:, PR_W12 % 2, 0:KD * DA].rearrange("p (c n) -> p c n", c=KD)
            copy(W12[:, :, 0, :], w12)
            copy(W12[:, :, 1, :], w12).then_inc(pr_free, 1)

            def weights(t):
                if t >= 2:
                    act.wait_ge(attq_full, 4 * (t - 1))
                if t == 0:
                    act.wait_ge(pr_free, PR_A2 + NQ)
                    act.wait_ge(nm_set, 1)
                nc.scalar.activation(att[:, t % 2, :], a2bc[:], ACT.Exp, bias=off1[:, t:t + 1])
                nc.scalar.activation(att2[:, t % 2, :], a2bc[:], ACT.Exp, bias=off2[:, t:t + 1],
                                     scale=ALPHA).then_inc(exp_set, 1)

            def adj_rows(t):
                act.wait_ge(adj_in[t % 3], 16 * (t // 3 + 1))
                if t >= 2:
                    act.wait_ge(rsum_set, t - 1)
                nc.scalar.activation(junk[:, t % 2, :], adjn[:, t % 3, :], ACT.Copy,
                                     accum_out=rsum[:, t:t + 1]).then_inc(rsum_set, 1)

            def elu_exp(t):
                act.wait_ge(ym_set, t + 1)
                nc.scalar.activation(tA[:, t % 2, :], tA[:, t % 2, :], ACT.Exp).then_inc(ee_set, 1)

            for t in range(H2_FIRST):
                h2_rows(t)
            weights(0)
            for t in range(H2_FIRST, NT):
                h2_rows(t)
            for t in range(NT):
                if 0 < t < NT - 1:
                    weights(t + 1)
                for q in range(4):
                    n = 4 * t + q
                    act.wait_ge(adjq_full, n + 1)
                    if t >= 2 and q == 0:
                        act.wait_ge(adjT_out[t % 2], 16 * (t // 2))
                    copy(adjT[:, t % 2, q * BANK:(q + 1) * BANK], tr[:, n % 2, :]).then_inc(adjq_free, 1)
                if t == 0:
                    weights(1)
                adj_rows(t)
                if t >= 2:
                    elu_exp(t - 2)
            roots(1)
            act.wait_ge(norm_set, 2)
            for t in range(*LN_PARTS[1]):
                normalise(t)
            elu_exp(NT - 2)
            elu_exp(NT - 1)
            nc.scalar.activation(lifted[:, 0, 0:2], ones[:], ACT.Sqrt)
            act.wait_ge(pr_full, PR_CS + 1)
            act.wait_ge(pr_free, PR_CS)
            copy(csum[:], pr[:, PR_CS % 2, 0:NT]).then_inc(pr_free, 1)

            act.wait_ge(colacc_set, NT)
            act.wait_ge(rsum_set, NT)
            for step in range(2):
                moved = 0
                for task in scalar_order(step):
                    kind, t = task[0], task[1]
                    if kind in ("lift_from", "lift", "steer"):
                        two = slice(2 * t, 2 * t + 2)
                        if kind == "lift_from":
                            act.wait_ge(l_free, step * NT + 2 * t + 2)
                            done.on(copy(aim[:, two], Zs[:, two], 2 * P_NUC))
                            moved = done.on(copy(nth[:, two], Zs[:, two], -LOW_END * RATIO[0]))
                            if LIFTS[step] == 0:
                                act.wait_ge(act_done, moved)
                                copy(nth[:, two], nth[:, two]).then_inc(lift_set, 1)
                        if kind == "lift":
                            e = E[:, t % SLOTS, :]
                            act.wait_ge(act_done, max(moved, done.n - 1))
                            done.on(nc.scalar.activation(lifted[:, 0, :], e, ACT.Relu, bias=nth[:, t:t + 1],
                                                         accum_out=above[:, t:t + 1]))
                            act.wait_ge(act_done, max(moved, done.n - 1))
                            done.on(nc.scalar.activation(lifted[:, 1, :], e, ACT.Sign, bias=nth[:, t:t + 1],
                                                         accum_out=signs[:, t:t + 1]))
                        if kind == "steer":
                            k = task[2]
                            up = RATIO[k + 1]
                            down = up / RATIO[k]
                            done.on(copy(nlift0[:, two], nth[:, two], (up + down) / 2))
                            done.on(copy(nlift1[:, two], nth[:, two], (down - up) / 2))
                            for i in (2 * t, 2 * t + 1):
                                one = slice(i, i + 1)
                                n = done.on(nc.scalar.activation(rest[:, one], nth[:, one], ACT.Identity,
                                                                 bias=aim[:, one], scale=float(N)))
                            for i in (2 * t, 2 * t + 1):
                                one = slice(i, i + 1)
                                act.wait_ge(act_done, n)
                                n2 = done.on(nc.scalar.activation(rest[:, one], above[:, one], ACT.Identity,
                                                                  bias=rest[:, one], scale=-2.0))
                            for i in (2 * t, 2 * t + 1):
                                one = slice(i, i + 1)
                                act.wait_ge(act_done, n2 - 1 + i % 2)
                                n3 = done.on(nc.scalar.activation(side_of[:, one], signs[:, one], ACT.Sign,
                                                                  bias=rest[:, one], scale=nth[:, one]))
                            for i in (2 * t, 2 * t + 1):
                                one = slice(i, i + 1)
                                act.wait_ge(act_done, n3 - 1 + i % 2)
                                moved = done.on(nc.scalar.activation(nth[:, one], side_of[:, one], ACT.Identity,
                                                                     bias=nlift0[:, one], scale=nlift1[:, one]))
                            if k + 1 == LIFTS[step]:
                                act.wait_ge(act_done, moved)
                                copy(nth[:, two], nth[:, two]).then_inc(lift_set, 1)
                        continue
                    key = (step, kind, t)
                    u, v, m = TRU[key], PRU[key], YU[key]
                    g = step * NT + t
                    if kind == "xt":
                        if t == 6:
                            act.wait_ge(norm_set, 3)
                            for i in range(*LN_PARTS[2]):
                                normalise(i)
                        flipped(u, t)
                    if kind in ("gk", "next_gk"):
                        if (kind, t) == ("gk", 0):
                            roots(2)
                            done.on(nc.scalar.activation(lifted[:, 0, 2:4], ones[:], ACT.Exp))
                        if kind == "next_gk":
                            act.wait_ge(l_full, NT)
                        act.wait_ge(pr_full, v + 1)
                        copy(GT[:, t * BANK:(t + 1) * BANK], pr[:, v % 2, :]).then_inc(pr_free, 1)
                        act.wait_ge(pr_full, v + 2)
                        half, col = t // 2, t % 2
                        part = slice(half * DA, (half + 1) * DA)
                        copy(KT[part, col * BANK:(col + 1) * BANK], pr[part, (v + 1) % 2, :]).then_inc(pr_free, 1)
                    if kind == "logits":
                        if g == 0:
                            for slot in range(2):
                                act.wait_ge(adjT_out[slot], 16 * NT // 2)
                        act.wait_ge(l_full, g + 1)
                        act.wait_ge(max_set, g + 1)
                        nc.scalar.activation(E[:, t % SLOTS, :], Lp[:].rearrange("p q n -> p (q n)"), ACT.Exp,
                                             bias=nmax[:, t:t + 1],
                                             accum_out=Zs[:, t:t + 1]).then_inc(l_free, 1)
                    if kind == "flip":
                        for q in range(4):
                            act.wait_ge(tr_full, u + q + 1)
                            copy(AT[:, t % 2, q * BANK:(q + 1) * BANK], tr[:, (u + q) % 2, :]).then_inc(tr_free, 1)
                    if kind == "spread" or kind == "mix" and step == 0:
                        k = items.index((kind, t))
                        act.wait_ge(pr_full, v + 1)
                        if kind == "mix":
                            act.wait_ge(rz_set, g // 2 + 1)
                        copy(nat[:, k % 2, :], pr[:, v % 2, 0:D],
                             rz[:, t:t + 1] if kind == "mix" else 1.0).then_inc(pr_free, 1)
                    if kind in ("turn_mix", "turn_spread"):
                        k = items.index((kind[5:], t))
                        act.wait_ge(tr_full, u + 1)
                        where = XT[:, :, t * P:(t + 1) * P] if kind == "turn_mix" else \
                            natT[:, k % 2, :].rearrange("p (c n) -> p c n", c=KD)
                        copy(where, tr[:, u % 2, 0:D].rearrange("p (c n) -> p c n", c=KD)).then_inc(tr_free, 1)
                    if kind in Y_KINDS[step] and m >= 2:
                        act.wait_ge(y_set, m - 1)
                    if kind == "use_mix":
                        act.wait_ge(pr_full, v + 1)
                        copy(yA[:, m % 2, 0:D], pr[:, v % 2, 0:D])
                        copy(V3[:, t, :], pr[:, v % 2, D:2 * D]).then_inc(pr_free, 1)
                    if kind == "mix" and step == 1:
                        if t == NT - 2:
                            roots(3)
                        act.wait_ge(pr_full, v + 1)
                        act.wait_ge(rz_set, g // 2 + 1)
                        nc.scalar.activation(yA[:, m % 2, 0:D], pr[:, v % 2, 0:D], ACT.Copy,
                                             scale=rz[:, t:t + 1]).then_inc(pr_free, 1)
                    if kind == "use_spread":
                        act.wait_ge(pr_full, v + 1)
                        if t == 0:
                            act.wait_ge(inv_set, 1)
                        for s, where in enumerate((yA[:, m % 2, :], V[:, t, :])):
                            act.wait_ge(pr_full, v + s + 1)
                            b = pr[:, (v + s) % 2, :]
                            copy(where[:, 0:D], b[:, 0:D], rinv[:, t:t + 1])
                            copy(where[:, D:2 * D], b[:, D:2 * D], cinv[:, t:t + 1]).then_inc(pr_free, 1)
                    if kind == "second":
                        act.wait_ge(pr_full, v + 1)
                        b = pr[:, v % 2, :]
                        copy(yA[:, m % 2, 0:D], b[:, 0:D], rinv[:, t:t + 1])
                        copy(yA[:, m % 2, D:2 * D], b[:, D:2 * D],
                             cinv[:, t:t + 1]).then_inc(pr_free, 1)
            roots(4)

        @block.tensor
        def _(pe):
            pe.wait_ge(consts_set, 2)

            def ring(free, n, depth=2):
                if n >= depth:
                    pe.wait_ge(free, n - depth + 1)

            def flip_rows(base, h_base, q):
                n = base + q
                pe.wait_ge(h_set, h_base + 2 * q + 2)
                ring(tr_free, n)
                for i in range(2):
                    for c in range(KD):
                        last = nc.tensor.transpose(tr[:, n % 2, (2 * c + i) * P:(2 * c + i + 1) * P],
                                                   Xn[:, 2 * q + i, c * P:(c + 1) * P], ident[:])
                last.then_inc(tr_full, 1)

            def a2_row(q):
                n = PR_A2 + q
                pe.wait_ge(wl_set, 2)
                pe.wait_ge(tr_free, TR_H + 2 * q + 2)
                ring(pr_free, n)
                for c in range(KD):
                    last = nc.tensor.matmul(pr[:, n % 2, :], wrb[:, c, :], XT[:, c, q * BANK:(q + 1) * BANK],
                                            start=c == 0, stop=c == KD - 1)
                last.then_inc(pr_full, 1)

            pe.wait_ge(wl_set, 1)
            for c in range(KD):
                last = nc.tensor.matmul(pr[:, PR_WL % 2, c * P:(c + 1) * P], wlb[:, c, :], ident[:],
                                        start=True, stop=True)
            last.then_inc(pr_full, 1)
            for c in range(4):
                for q in (2 * c, 2 * c + 1):
                    flip_rows(TR_H, 0, q)
                if c:
                    a2_row(c - 1)
            a2_row(3)
            pe.wait_ge(w1_in, 16 * 10)
            ring(tr_free, TR_W1)
            for c in range(KD):
                last = nc.tensor.transpose(tr[0:DA, TR_W1 % 2, c * P:(c + 1) * P], W1s[:, c, :], ident[:])
            last.then_inc(tr_full, 1)
            pe.wait_ge(tr_free, TR_W1 + 1)
            ring(pr_free, PR_W12)
            for c in range(KD):
                last = nc.tensor.matmul(pr[:, PR_W12 % 2, c * DA:(c + 1) * DA], W1T[:, c * P:(c + 1) * P], W2s,
                                        start=True, stop=True)
            last.then_inc(pr_full, 1)
            for t in range(NT):
                n = PR_H2 + t
                ring(pr_free, n)
                for c in range(KD):
                    last = nc.tensor.matmul(pr[:, n % 2, 0:D], XT[:, c, t * P:(t + 1) * P], We[:, c, 0:D],
                                            start=c == 0, stop=c == KD - 1)
                last.then_inc(pr_full, 1)

            def adj_flip(t, q):
                n = 4 * t + q
                if n < 2:
                    pe.wait_ge(tr_free, TR_W1 + 1)
                pe.wait_ge(adj_in[t % 3], 16 * (t // 3 + 1))
                ring(adjq_free, n)
                for i in range(4):
                    j = (4 * q + i) * P
                    last = nc.tensor.transpose(tr[:, n % 2, i * P:(i + 1) * P], adjn[:, t % 3, j:j + P], ident[:])
                last.then_inc(adjq_full, 1)

            def att_flips(t):
                pe.wait_ge(att_set, t + 1)
                for q in range(4):
                    n = 4 * t + q
                    ring(attq_free, n, 4)
                    for i in range(4):
                        j = (4 * q + i) * P
                        last = nc.tensor.transpose(Lp[:, q, i * P:(i + 1) * P], att[:, t % 2, j:j + P], ident[:])
                    last.then_inc(attq_full, 1)

            def product(n, panel, right, width):
                ring(pr_free, n)
                for j in range(NT):
                    last = nc.tensor.matmul(pr[:, n % 2, 0:width], panel[:, j * P:(j + 1) * P], right[:, j, 0:width],
                                            start=j == 0, stop=j == NT - 1)
                last.then_inc(pr_full, 1)

            for q in range(4):
                adj_flip(0, q)
            att_flips(0)
            for t in range(NT):
                if 0 < t < NT - 1:
                    att_flips(t + 1)
                n = PR_Y + t
                pe.wait_ge(attq_free, 4 * (t + 1))
                if t == 0:
                    pe.wait_ge(pr_free, PR_Y)
                ring(pr_free, n)
                for j in range(NT):
                    if t + 1 < NT and j % 4 == 2:
                        adj_flip(t + 1, j // 4)
                    last = nc.tensor.matmul(pr[:, n % 2, 0:D], attT[:, t % 2, j * P:(j + 1) * P], h2[:, j, 0:D],
                                            start=j == 0, stop=j == NT - 1)
                last.then_inc(pr_full, 1)
                if t == 0:
                    att_flips(1)
            pe.wait_ge(adjq_free, 4 * NT)
            pe.wait_ge(colacc_set, NT)
            ring(pr_free, PR_CS)
            for j in range(NT):
                last = nc.tensor.matmul(pr[:, PR_CS % 2, j:j + 1], colacc[:, j * P:(j + 1) * P], ones[:, 0:1],
                                        start=True, stop=True)
            last.then_inc(pr_full, 1)

            np_ = [0]
            for step in range(2):
                for kind, t in ORDER[step]:
                    key = (step, kind, t)
                    u, v = TRU[key], PRU[key]
                    g = step * NT + t
                    if kind == "xt":
                        flip_rows(u - t, NT, t)
                    if kind in ("gk", "next_gk"):
                        whole = ("xt", 2 * t + 1) if kind == "gk" else ("turn_mix", 4 * t + 3)
                        pe.wait_ge(tr_free, TRU[(0,) + whole] + 1)
                        for i, w in enumerate((W12, W3s)):
                            ring(pr_free, v + i)
                            for c in range(KD):
                                last = nc.tensor.matmul(pr[:, (v + i) % 2, :], w[:, c, :, :].rearrange("p a b -> p (a b)"),
                                                        XT[:, c, t * BANK:(t + 1) * BANK],
                                                        start=c == 0, stop=c == KD - 1)
                            last.then_inc(pr_full, 1)
                    if kind == "logits":
                        if g:
                            pe.wait_ge(l_free, g)
                        if t == 0:
                            pe.wait_ge(pr_free, GK_DONE[step])
                        for q in (0, 2, 1, 3):
                            part = slice(q // 2 * DA, (q // 2 + 1) * DA)
                            last = nc.tensor.matmul(Lp[:, q, :], GT[part, t * P:(t + 1) * P],
                                                    KT[part, q % 2 * BANK:(q % 2 + 1) * BANK],
                                                    start=True, stop=True)
                        last.then_inc(l_full, 1)
                    if kind == "flip":
                        pe.wait_ge(keep_set, g + 1)
                        for q in range(4):
                            ring(tr_free, u + q)
                            for i in range(4):
                                j = (4 * q + i) * P
                                last = nc.tensor.transpose(tr[:, (u + q) % 2, i * P:(i + 1) * P],
                                                           E[:, t % SLOTS, j:j + P], ident[:])
                            last.then_inc(tr_full, 1)
                    if kind == "mix":
                        pe.wait_ge(tr_free, TRU[(step, "flip", t)] + 4)
                        product(v, AT[:, t % 2, :], V3 if step else Xn, D)
                    if kind == "spread":
                        pe.wait_ge(st_in[np_[0] % 2], 16 * (np_[0] // 2 + 1))
                        product(v, ST[:, np_[0] % 2, :], Xn, D)
                        np_[0] += 1
                    if kind == "second":
                        pe.wait_ge(pr_free, PRU[(0, "use_spread", NT - 1)] + 2)
                        pe.wait_ge(st_in[np_[0] % 2], 16 * (np_[0] // 2 + 1))
                        product(v, ST[:, np_[0] % 2, :], V, 2 * D)
                        np_[0] += 1
                    if kind in ("turn_mix", "turn_spread"):
                        product_key = (0, kind[5:], t)
                        k = items.index(product_key[1:])
                        pe.wait_ge(pr_free, PRU[product_key] + 1)
                        ring(tr_free, u)
                        for c in range(KD):
                            last = nc.tensor.transpose(tr[:, u % 2, c * P:(c + 1) * P], nat[:, k % 2, c * P:(c + 1) * P],
                                                       ident[:])
                        last.then_inc(tr_full, 1)
                    if kind in ("use_mix", "use_spread"):
                        turn = "turn_" + kind[4:]
                        k = items.index((kind[4:], t))
                        pe.wait_ge(tr_free, TRU[(0, turn, t)] + 1)
                        for s in range(1 if kind == "use_mix" else 2):
                            ring(pr_free, v + s)
                            for c in range(KD):
                                if kind == "use_mix":
                                    left, right = XT[:, c, t * P:(t + 1) * P], U3s[:, c, :]
                                else:
                                    left, right = natT[:, k % 2, c * P:(c + 1) * P], U12s[:, c, s, :]
                                last = nc.tensor.matmul(pr[:, (v + s) % 2, :], left, right,
                                                        start=c == 0, stop=c == KD - 1)
                            last.then_inc(pr_full, 1)

        @block.vector
        def _(dve):
            done = Tally(vec_done)

            def link(ins):
                done.on(ins)
                dve.wait_ge(vec_done, done.n)

            def stats(tiles, ready=None):
                for t in tiles:
                    if ready:
                        ready(t)
                    n = done.on(nc.vector.bn_stats(st6[:, t, :], Xb[:, t, :]))
                    if t > tiles[0]:
                        dve.wait_ge(vec_done, n - 1)
                        n = done.on(nc.vector.bn_aggr(mv[:, t - 1, :], st6[:, t - 1, :]))
                dve.wait_ge(vec_done, done.n)
                link(nc.vector.bn_aggr(mv[:, tiles[-1], :], st6[:, tiles[-1], :]))

            def scales(n, shift=True):
                a, b = LN_PARTS[n]
                part = slice(a, b)
                nc.vector.tensor_scalar(out=ve[:, part], in0=mv[:, part, 1], scalar1=EPS_LN, scalar2=None,
                                        op0=ALU.add).then_inc(var_set, 1)
                dve.wait_ge(sqrt_set, n + 1)
                link(nc.vector.reciprocal(y0[:, part], sd[:, part]))
                link(nc.vector.tensor_tensor(out=yt[:, part], in0=y0[:, part], in1=y0[:, part], op=ALU.mult))
                link(nc.vector.tensor_tensor(out=yt[:, part], in0=yt[:, part], in1=ve[:, part], op=ALU.mult))
                link(nc.vector.tensor_scalar(out=yt[:, part], in0=yt[:, part], scalar1=-0.5, scalar2=1.5,
                                             op0=ALU.mult, op1=ALU.add))
                link(nc.vector.tensor_tensor(out=rstd[:, part], in0=y0[:, part], in1=yt[:, part], op=ALU.mult))
                if shift:
                    nc.vector.scalar_tensor_tensor(out=nmr[:, part], in0=mv[:, part, 0], scalar=-1.0,
                                                   in1=rstd[:, part], op0=ALU.mult, op1=ALU.mult).then_inc(norm_set, 1)

            dve.wait_ge(w0_in, 48)
            for i in range(2):
                for c in range(KD):
                    link(nc.vector.scalar_tensor_tensor(out=wjunk, in0=We[:, c, 0:D], scalar=1.0,
                                                        in1=albc[:, i, :], op0=ALU.mult, op1=ALU.mult,
                                                        accum_out=We[:, c, D + i:D + i + 1]))
            for i, w in enumerate((wlb, wrb)):
                link(nc.vector.memset(w, 1.0))
                for c in range(KD):
                    last = nc.vector.tensor_scalar(out=w[:, c, :], in0=w[:, c, :], scalar1=We[:, c, D + i:D + i + 1],
                                                   scalar2=None, op0=ALU.mult)
                last.then_inc(wl_set, 1)
            stats(range(NT), lambda t: dve.wait_ge(x_in[t * 4 // NT], 16))
            scales(0)
            dve.wait_ge(pr_free, PR_WL + 1)
            for t in range(NT):
                dve.wait_ge(h_set, t + 1)
                if t >= 2:
                    dve.wait_ge(vec_done, done.n - 1)
                done.on(nc.vector.scalar_tensor_tensor(out=a1junk[:, t % 2, :], in0=Xn[:, t, :], scalar=1.0,
                                                       in1=wlbc, op0=ALU.mult, op1=ALU.mult,
                                                       accum_out=h2[:, t, D:D + 1]))
            dve.wait_ge(vec_done, done.n)
            dve.wait_ge(pr_free, PR_A2 + NQ)
            link(nc.vector.reduce_max(a2max[:], a2bc[:], axis=AX))
            link(nc.vector.tensor_scalar(out=sm[:], in0=h2[:, :, D], scalar1=a2max[:], scalar2=None, op0=ALU.add))
            link(nc.vector.tensor_scalar(out=sm2[:], in0=sm[:], scalar1=ALPHA, scalar2=None, op0=ALU.mult))
            link(nc.vector.tensor_tensor(out=sm[:], in0=sm[:], in1=sm2[:], op=ALU.max))
            done.on(nc.vector.tensor_tensor(out=off1[:], in0=h2[:, :, D], in1=sm[:], op=ALU.subtract))
            nc.vector.scalar_tensor_tensor(out=off2[:], in0=h2[:, :, D], scalar=ALPHA, in1=sm[:], op0=ALU.mult,
                                           op1=ALU.subtract).then_inc(nm_set, 1)

            def elu_parts(t):
                n = PR_Y + t
                dve.wait_ge(pr_full, n + 1)
                if t >= 2:
                    dve.wait_ge(ee_set, t - 1)
                nc.vector.tensor_scalar(out=tA[:, t % 2, :], in0=pr[:, n % 2, 0:D], scalar1=rden[:, t:t + 1],
                                        scalar2=0.0, op0=ALU.mult, op1=ALU.min).then_inc(ym_set, 1)
                nc.vector.tensor_scalar(out=tB[:, t % 2, :], in0=pr[:, n % 2, 0:D], scalar1=rden[:, t:t + 1],
                                        scalar2=0.0, op0=ALU.mult, op1=ALU.max).then_inc(pr_free, 1)

            def residual(t):
                dve.wait_ge(ee_set, t + 1)
                dve.wait_ge(pr_free, PR_Y + t + 1)
                link(nc.vector.scalar_tensor_tensor(out=tB[:, t % 2, :], in0=tA[:, t % 2, :], scalar=-1.0,
                                                    in1=tB[:, t % 2, :], op0=ALU.add, op1=ALU.add))
                nc.vector.tensor_tensor(out=Xb[:, t, :], in0=Xb[:, t, :], in1=tB[:, t % 2, :],
                                        op=ALU.add).then_inc(x1_set, 1)
                dve.wait_ge(x1_set, t + 1)
                stats(range(t, t + 1))

            for t in range(NT + 3):
                if t < NT:
                    a = att[:, t % 2, :]
                    dve.wait_ge(exp_set, t + 1)
                    dve.wait_ge(adj_in[t % 3], 16 * (t // 3 + 1))
                    link(nc.vector.tensor_tensor(out=a, in0=a, in1=att2[:, t % 2, :], op=ALU.max))
                    nc.vector.scalar_tensor_tensor(out=a, in0=a, scalar=1.0, in1=adjn[:, t % 3, :], op0=ALU.mult,
                                                   op1=ALU.mult, accum_out=deno[:, t:t + 1]).then_inc(att_set, 1)
                    dve.wait_ge(att_set, t + 1)
                    link(nc.vector.tensor_scalar(out=rden[:, t:t + 1], in0=deno[:, t:t + 1], scalar1=EPS_ATT,
                                                 scalar2=None, op0=ALU.add))
                    done.on(nc.vector.reciprocal(rden[:, t:t + 1], rden[:, t:t + 1]))
                    for q in range(4):
                        n = 4 * t + q
                        dve.wait_ge(attq_full, n + 1)
                        if t >= 2 and q == 0:
                            dve.wait_ge(pr_full, PR_Y + t - 1)
                        nc.vector.tensor_copy(attT[:, t % 2, q * BANK:(q + 1) * BANK],
                                              Lp[:, q, :]).then_inc(attq_free, 1)
                if t == NT:
                    scales(1)
                if 2 <= t < NT + 2:
                    elu_parts(t - 2)
                if t >= 3:
                    residual(t - 3)
            scales(2)
            dve.wait_ge(pr_free, PR_CS + 1)
            dve.wait_ge(rsum_set, NT)
            for total, inverse in ((rsum, rinv), (csum, cinv)):
                link(nc.vector.tensor_scalar(out=inverse[:], in0=total[:], scalar1=1.0, scalar2=1e-12,
                                             op0=ALU.add, op1=ALU.max))
                last = nc.vector.reciprocal(inverse[:], inverse[:])
            last.then_inc(inv_set, 1)

            for k in range(STEPS):
                up = RATIO[k + 1] if k + 1 < STEPS else 1.0
                nc.vector.memset(ups[:, k:k + 1], up - up / RATIO[k])
                tables = done.on(nc.vector.memset(downs[:, k:k + 1], up / RATIO[k]))

            def bisect(i, first, unread, rows_of):
                two = slice(2 * i, 2 * i + 2)
                with dve.Fori(first, STEPS, 1) as k:
                    dve.sem_clear(slow_done)
                    for t in (2 * i, 2 * i + 1):
                        nc.vector.scalar_tensor_tensor(out=unread(t), in0=rows_of(t), scalar=th[:, t:t + 1],
                                                       in1=rows_of(t), op0=ALU.is_gt, op1=ALU.mult,
                                                       accum_out=Ms[:, t:t + 1]).then_inc(slow_done, 1)
                    dve.wait_ge(slow_done, 2)
                    nc.vector.tensor_tensor(out=cs[:, two], in0=Ms[:, two], in1=Ts[:, two],
                                            op=ALU.is_ge).then_inc(slow_done, 1)
                    dve.wait_ge(slow_done, 3)
                    nc.vector.tensor_scalar(out=fs[:, two], in0=cs[:, two], scalar1=ups[:, bass.ds(k, 1)],
                                            scalar2=downs[:, bass.ds(k, 1)], op0=ALU.mult,
                                            op1=ALU.add).then_inc(slow_done, 1)
                    dve.wait_ge(slow_done, 4)
                    nc.vector.tensor_tensor(out=th[:, two], in0=th[:, two], in1=fs[:, two],
                                            op=ALU.mult).then_inc(slow_done, 1)
                    dve.wait_ge(slow_done, 5)

            def take(i, flags):
                two = slice(2 * i, 2 * i + 2)
                dve.sem_clear(slow_done)
                nc.vector.tensor_scalar(out=fs[:, two], in0=flags[:, two], scalar1=0.0, scalar2=None,
                                        op0=ALU.is_equal).then_inc(slow_done, 1)
                dve.wait_ge(slow_done, 1)
                nc.vector.tensor_tensor(out=cut[:, two], in0=cut[:, two], in1=fs[:, two],
                                        op=ALU.mult).then_inc(slow_done, 1)
                dve.wait_ge(slow_done, 2)
                nc.vector.tensor_tensor(out=cut[:, two], in0=cut[:, two], in1=th[:, two],
                                        op=ALU.max).then_inc(slow_done, 1)
                dve.wait_ge(slow_done, 3)

            def whole_rows(i):
                two = slice(2 * i, 2 * i + 2)
                dve.sem_clear(slow_done)
                nc.vector.tensor_scalar(out=Ts[:, two], in0=Zs[:, two], scalar1=P_NUC, scalar2=None,
                                        op0=ALU.mult).then_inc(slow_done, 1)
                nc.vector.tensor_scalar(out=th[:, two], in0=Zs[:, two], scalar1=LOW_END * RATIO[0], scalar2=None,
                                        op0=ALU.mult).then_inc(slow_done, 1)
                dve.wait_ge(slow_done, 2)
                bisect(i, 0, lambda t: junk[:, t % 2, :], lambda t: E[:, t % SLOTS, :])
                take(i, lost)

            junk_free, junk2_free = [done.n, done.n], [done.n, done.n]
            dve.wait_ge(vec_done, tables)
            link(nc.vector.memset(st6[:], 0.0))
            for step in range(2):
                coarse = COARSE[step]
                probed, compared, factored, moved = {}, {}, {}, {}
                for unit in search_units(step):
                    kind, i = unit[0], unit[1]
                    two = slice(2 * i, 2 * i + 2)
                    if kind == "max":
                        g = step * NT + i
                        dve.wait_ge(l_full, g + 1)
                        nc.vector.reduce_max(nmax[:, i:i + 1], Lp[:].rearrange("p q n -> p (q n)"), axis=AX,
                                             negate=True).then_inc(max_set, 1)
                    if kind == "begin":
                        dve.wait_ge(l_free, step * NT + 2 * i + 2)
                        done.on(nc.vector.tensor_scalar(out=Ts[:, two], in0=Zs[:, two], scalar1=P_NUC, scalar2=None,
                                                        op0=ALU.mult))
                        start, factor = Zs, LOW_END * RATIO[0]
                        if i > 0:
                            dve.wait_ge(lift_set, step * (NT // 2 - 1) + i)
                            start, factor = nth, -1.0
                        moved[i] = done.on(nc.vector.tensor_scalar(out=th[:, two], in0=start[:, two],
                                                                   scalar1=factor, scalar2=None, op0=ALU.mult))
                    if kind == "probe":
                        e = E[:, i % SLOTS, :]
                        dve.wait_ge(vec_done, max(moved[i // 2], junk_free[i % 2]))
                        probed[i // 2] = junk_free[i % 2] = done.on(nc.vector.scalar_tensor_tensor(
                            out=junk[:, i % 2, :], in0=e, scalar=th[:, i:i + 1], in1=e, op0=ALU.is_gt, op1=ALU.mult,
                            accum_out=Ms[:, i:i + 1]))
                    if kind == "fine":
                        c = cand[:, i % 2, :]
                        dve.wait_ge(vec_done, max(moved[i // 2], junk2_free[i % 2]))
                        probed[i // 2] = junk2_free[i % 2] = done.on(nc.vector.scalar_tensor_tensor(
                            out=junk2[:, i % 2, :], in0=c, scalar=th[:, i:i + 1], in1=c, op0=ALU.is_gt, op1=ALU.mult,
                            accum_out=Ms[:, i:i + 1]))
                    if kind == "compare":
                        dve.wait_ge(vec_done, probed[i])
                        compared[i] = done.on(nc.vector.tensor_tensor(out=cs[:, two], in0=Ms[:, two], in1=Ts[:, two],
                                                                      op=ALU.is_ge))
                    if kind == "factor":
                        k = unit[2]
                        up = RATIO[k + 1] if k + 1 < STEPS else 1.0
                        down = up / RATIO[k]
                        dve.wait_ge(vec_done, compared[i])
                        factored[i] = done.on(nc.vector.tensor_scalar(out=fs[:, two], in0=cs[:, two],
                                                                      scalar1=up - down, scalar2=down,
                                                                      op0=ALU.mult, op1=ALU.add))
                    if kind == "move":
                        dve.wait_ge(vec_done, factored[i])
                        moved[i] = done.on(nc.vector.tensor_tensor(out=th[:, two], in0=th[:, two], in1=fs[:, two],
                                                                   op=ALU.mult))
                    if kind == "collect":
                        if i % 2 == 0:
                            two = slice(i, i + 2)
                            dve.wait_ge(vec_done, moved[i // 2])
                            upper = done.on(nc.vector.tensor_scalar(out=hi[:, two], in0=th[:, two],
                                                                    scalar1=RATIO[coarse] * MARGIN, scalar2=None,
                                                                    op0=ALU.mult))
                            dve.wait_ge(vec_done, upper)
                        for half in range(2):
                            e = E[:, i % SLOTS, half * N // 2:(half + 1) * N // 2]
                            dve.wait_ge(vec_done, max(junk_free))
                            masked = done.on(nc.vector.scalar_tensor_tensor(
                                out=mbuf[:], in0=e, scalar=hi[:, i:i + 1], in1=e, op0=ALU.is_le, op1=ALU.mult,
                                accum_out=tails[:, half, i:i + 1]))
                            dve.wait_ge(vec_done, masked)
                            for j in range(NSEG // 2):
                                first = (half * NSEG // 2 + j) * 8
                                collected = done.on(nc.vector.max(out=cand[:, i % 2, first:first + 8],
                                                                  in_=mbuf[:, j * SEG:(j + 1) * SEG]))
                            junk_free = [collected, collected]
                    if kind == "resolve":
                        pair = step * NT // 2 + i
                        dve.wait_ge(vec_done, collected)
                        link(nc.vector.tensor_tensor(out=Ts[:, two], in0=tails[:, 0, two], in1=tails[:, 1, two],
                                                     op=ALU.add))
                        done.on(nc.vector.scalar_tensor_tensor(out=Ts[:, two], in0=Zs[:, two], scalar=P_NUC - 1,
                                                               in1=Ts[:, two], op0=ALU.mult, op1=ALU.add))
                        link(nc.vector.reduce_max(
                            eighth[:, two], cand[:].rearrange("p s (g e) -> p s g e", e=8)[:, :, :, 7],
                            axis=AX))
                        done.on(nc.vector.scalar_tensor_tensor(out=lost[:, two], in0=eighth[:, two],
                                                               scalar=RATIO[coarse] * MARGIN, in1=th[:, two],
                                                               op0=ALU.mult, op1=ALU.is_ge))
                    if kind == "finish":
                        pair = step * NT // 2 + i
                        dve.wait_ge(vec_done, moved[i])
                        link(nc.vector.tensor_scalar(out=hi[:, two], in0=th[:, two],
                                                     scalar1=RATIO[FINE[step]] * MARGIN, scalar2=None, op0=ALU.mult))
                        for t in (2 * i, 2 * i + 1):
                            c = cand[:, t % 2, :]
                            dve.wait_ge(vec_done, junk2_free[t % 2])
                            junk2_free[t % 2] = done.on(nc.vector.scalar_tensor_tensor(
                                out=junk2[:, t % 2, :], in0=c, scalar=hi[:, t:t + 1], in1=c, op0=ALU.is_gt,
                                op1=ALU.mult, accum_out=Ms[:, t:t + 1]))
                        for t in (2 * i, 2 * i + 1):
                            c = cand[:, t % 2, :]
                            dve.wait_ge(vec_done, junk2_free[t % 2])
                            masked = done.on(nc.vector.scalar_tensor_tensor(out=c, in0=c, scalar=hi[:, t:t + 1], in1=c,
                                                                            op0=ALU.is_le, op1=ALU.mult))
                        for t in (2 * i, 2 * i + 1):
                            dve.wait_ge(vec_done, masked - 1 + t % 2)
                            tops = done.on(nc.vector.max(out=top8[:, t % 2, 8:16], in_=cand[:, t % 2, :]))
                        done.on(nc.vector.tensor_tensor(out=Ts[:, two], in0=Ts[:, two], in1=Ms[:, two],
                                                        op=ALU.subtract))
                        dve.wait_ge(vec_done, tops)
                        n = done.on(nc.vector.tensor_tensor(out=sum2[:, :, 8:16], in0=top8[:, :, 8:16],
                                                            in1=top8[:, :, 7:15], op=ALU.add))
                        dve.wait_ge(vec_done, n - 1)
                        done.on(nc.vector.tensor_scalar(out=Ts[:, two], in0=Ts[:, two], scalar1=1e-30, scalar2=None,
                                                        op0=ALU.max))
                        dve.wait_ge(vec_done, n)
                        link(nc.vector.tensor_tensor(out=sum4[:, :, 8:16], in0=sum2[:, :, 8:16],
                                                     in1=sum2[:, :, 6:14], op=ALU.add))
                        link(nc.vector.tensor_tensor(out=sum2[:, :, 8:16], in0=sum4[:, :, 8:16],
                                                     in1=sum4[:, :, 4:12], op=ALU.add))
                        n2 = done.on(nc.vector.tensor_tensor(
                            out=sum4[:, :, 8:16], in0=sum2[:, :, 7:15],
                            in1=Ts[:, two].rearrange("p (s o) -> p s o", o=1).to_broadcast([P, 2, 8]), op=ALU.is_ge))
                        dve.wait_ge(vec_done, n2)
                        n2 = done.on(nc.vector.scalar_tensor_tensor(out=sum4[:, :, 8:16], in0=sum4[:, :, 8:16],
                                                                    scalar=-4.0, in1=top8[:, :, 8:16], op0=ALU.mult,
                                                                    op1=ALU.subtract))
                        dve.wait_ge(vec_done, n2)
                        cut_set = done.on(nc.vector.reduce_max(cut[:, two], sum4[:, :, 8:16], axis=AX, negate=True))
                        dve.wait_ge(vec_done, cut_set)
                        for t in (2 * i, 2 * i + 1):
                            c = cand[:, t % 2, :]
                            junk2_free[t % 2] = done.on(nc.vector.scalar_tensor_tensor(
                                out=junk2[:, t % 2, :], in0=c, scalar=cut[:, t:t + 1], in1=c, op0=ALU.is_ge,
                                op1=ALU.mult, accum_out=Ms[:, t:t + 1]))
                        dve.wait_ge(vec_done, max(junk2_free))
                        link(nc.vector.scalar_tensor_tensor(out=eighth[:, two], in0=Ms[:, two], scalar=MARGIN,
                                                            in1=Ts[:, two], op0=ALU.mult, op1=ALU.is_lt))
                        link(nc.vector.scalar_tensor_tensor(out=lost[:, two], in0=lost[:, two], scalar=2.0,
                                                            in1=eighth[:, two], op0=ALU.mult, op1=ALU.max))
                        nc.vector.reduce_max(lost_pair[:, pair:pair + 1], lost[:, two], axis=AX).then_inc(lost_set, 1)
                    if kind == "check":
                        pair = step * NT // 2 + i
                        dve.wait_ge(any_set, pair + 1)
                        any_lost = dve.value_load(lost_any[0:1, pair:pair + 1], min_val=0, max_val=2)
                        with dve.If(any_lost > 0):
                            dve.wait_ge(vec_done, max(cut_set, *junk2_free))
                            bisect(i, FINE[step], lambda t: junk2[:, t % 2, :], lambda t: cand[:, t % 2, :])
                            take(i, eighth)
                            with dve.If(any_lost > 1):
                                dve.wait_ge(vec_done, max(junk_free))
                                whole_rows(i)
                    if kind == "keep":
                        dve.wait_ge(vec_done, cut_set)
                        for t in (2 * i, 2 * i + 1):
                            e = E[:, t % SLOTS, :]
                            nc.vector.scalar_tensor_tensor(out=e, in0=e, scalar=cut[:, t:t + 1], in1=e, op0=ALU.is_ge,
                                                           op1=ALU.mult, accum_out=Zk[:, t:t + 1]).then_inc(keep_set, 1)
                        dve.wait_ge(keep_set, step * NT + 2 * i + 2)
                        nc.vector.reciprocal(rz[:, two], Zk[:, two]).then_inc(rz_set, 1)
            def finished(n):
                a, b = LN_PARTS[n]
                stats(range(a, b), lambda t: dve.wait_ge(y_set, YU[(1, "mix", t)] + 1))
                scales(n, shift=False)
                dve.wait_ge(x1_in, 48)
                for t in range(a, b + 1):
                    if t < b:
                        n = done.on(nc.vector.scalar_tensor_tensor(
                            out=Xb[:, t, :], in0=Xb[:, t, :], scalar=mv[:, t, 0:1], in1=gam, op0=ALU.subtract,
                            op1=ALU.mult))
                    if t > a:
                        dve.wait_ge(xb_set, t)
                        dve.wait_ge(vec_done, n - (t < b))
                        nc.vector.scalar_tensor_tensor(
                            out=Xb[:, t - 1, :], in0=Xb[:, t - 1, :], scalar=rstd[:, t - 1:t],
                            in1=x1r[:, (t - 1) * D:t * D], op0=ALU.mult, op1=ALU.add).then_inc(out_set, 1)

            finished(3)
            finished(4)


_INS = ["x", "adj", "L0_gnn_W", "L0_gnn_attn_l", "L0_gnn_attn_r", "L1_gnn_W1", "L1_gnn_W2", "L1_gnn_W3",
        "L1_gnn_U1", "L1_gnn_U2", "L1_gnn_U3", "L1_gnn_gamma", "L1_gnn_beta"]


def kernel(**inputs):
    import numpy as np
    import concourse.bacc as bacc
    from concourse.bass_utils import run_bass_kernel_spmd

    nc = bacc.Bacc("TRN2", target_bir_lowering=False, num_devices=1)
    arrays, args = {}, []
    for name in _INS:
        a = np.ascontiguousarray(inputs[name])
        arrays[f"in_{name}"] = a
        args.append(nc.dram_tensor(f"in_{name}", a.shape, mybir.dt.from_np(a.dtype), kind="ExternalInput").ap())
    out = nc.dram_tensor("out", (N, D), mybir.dt.float32, kind="ExternalOutput").ap()
    build(nc, *args, out)
    r = run_bass_kernel_spmd(nc, [arrays], core_ids=[0])
    return r.results[0]["out"]
```
